# Optimizing a Trainium2 kernel written in Bass

```python
import numpy as np
import jax
import jax.numpy as jnp

def _softmax(x, axis=-1):
    return jax.nn.softmax(x, axis=axis)

def _gelu(x):
    return jax.nn.gelu(x, approximate=True)

def _silu(x):
    return jax.nn.silu(x)

def _sigmoid(x):
    return jax.nn.sigmoid(x)

def _layernorm(x, axis=-1, eps=1e-05):
    m = jnp.mean(x, axis=axis, keepdims=True)
    v = jnp.var(x, axis=axis, keepdims=True)
    return (x - m) / jnp.sqrt(v + eps)

def _scatter_add(tgt, idx, src, axis=0):
    return tgt.at[idx].add(src)

def _segment_sum(src, seg, n):
    return jax.ops.segment_sum(src, seg, n)
kernel_name = 'mk_gnn_resnorm_d1_gnn_r8_120e50'

def setup_inputs(seed: int=0):
    np.random.seed(seed)
    _w = jnp.asarray

    def _rec_inputs():
        import jax
        import jax.numpy as jnp
        _gk = jax.random.key(seed)
        x = -0.000202 + 1 * jax.random.normal(jax.random.fold_in(_gk, 1), (6250, 128), jnp.float32)
        src = jax.random.randint(jax.random.fold_in(_gk, 2), (100000,), 0, 6250, jnp.int32)
        dst = jnp.minimum((6250 * jax.random.uniform(jax.random.fold_in(_gk, 3), (100000,)) ** 2.0).astype(jnp.int32), 49999)
        _o = jnp.argsort(dst, stable=True)
        src = src[_o]
        dst = dst[_o]
        edge_attr_128 = -8.16379e-05 + 0.999858 * jax.random.normal(jax.random.fold_in(_gk, 12), (100000, 128), jnp.float32)
        return (x, src, dst, edge_attr_128)
    x, src, dst, edge_attr_128 = _rec_inputs()

    def _L0_gnn_setup():
        import jax, jax.numpy as jnp
        import numpy as np
        N, E, D = (6250, 100000, 128)
        SLOPE = 0.2
        key = jax.random.key(seed)
        ks = jax.random.split(key, 8)
        x = jax.random.normal(ks[0], (N, D), dtype=jnp.float32)
        alpha = jax.random.normal(ks[1], (E, D), dtype=jnp.float32)
        Wl = jax.random.normal(ks[2], (D, D), dtype=jnp.float32) / np.sqrt(D).astype(np.float32)
        bl = jax.random.normal(ks[3], (D,), dtype=jnp.float32) * 0.01
        Wr = jax.random.normal(ks[4], (D, D), dtype=jnp.float32) / np.sqrt(D).astype(np.float32)
        br = jax.random.normal(ks[5], (D,), dtype=jnp.float32) * 0.01
        src = jax.random.randint(ks[6], (E,), 0, N, dtype=jnp.int64)
        dst = jax.random.randint(ks[7], (E,), 0, N, dtype=jnp.int64)
        return {'x': x, 'alpha': alpha, 'Wl': Wl, 'bl': bl, 'Wr': Wr, 'br': br, 'src': src, 'dst': dst}
    _L0_gnn_all = _L0_gnn_setup()
    _L0_gnn_in = {k: v for k, v in _L0_gnn_all.items() if k in ('Wl', 'bl', 'Wr', 'br')}
    del _L0_gnn_all
    return {'x': x, 'src': src, 'dst': dst, 'edge_attr_128': edge_attr_128, 'L0_gnn_Wl': _L0_gnn_in['Wl'], 'L0_gnn_bl': _L0_gnn_in['bl'], 'L0_gnn_Wr': _L0_gnn_in['Wr'], 'L0_gnn_br': _L0_gnn_in['br']}

def reference(x, src, dst, edge_attr_128, L0_gnn_Wl, L0_gnn_bl, L0_gnn_Wr, L0_gnn_br):
    import jax
    import jax.numpy as jnp

    def _L0_gnn_ref(x, alpha, Wl, bl, Wr, br, src, dst):
        import jax, jax.numpy as jnp
        import numpy as np
        N, E, D = (6250, 100000, 128)
        SLOPE = 0.2
        n_nodes = x.shape[0]
        hl = x @ Wl.T + bl
        hr = x @ Wr.T + br
        s = (jnp.take(hl, src, axis=0) + jnp.take(hr, dst, axis=0)) * alpha
        s = jnp.where(s >= 0, s, SLOPE * s)
        smax = jax.ops.segment_max(s, dst, num_segments=n_nodes)
        e = jnp.exp(s - jnp.take(smax, dst, axis=0))
        denom = jax.ops.segment_sum(e, dst, num_segments=n_nodes)
        att = e / jnp.take(denom, dst, axis=0)
        msg = jnp.take(x, src, axis=0) * att
        return jax.ops.segment_sum(msg, dst, num_segments=n_nodes)
    x = _layernorm(x + _L0_gnn_ref(x, edge_attr_128, L0_gnn_Wl, L0_gnn_bl, L0_gnn_Wr, L0_gnn_br, src, dst), axis=-1)
    return x

_drawn_inputs = setup_inputs


def setup_inputs(seed=0):
    import zlib

    import numpy as np

    out = dict(_drawn_inputs(seed))
    spreads = {}
    factors = {'L0_gnn_bl': 8.0, 'L0_gnn_br': 8.0}
    for name, (base, spread) in spreads.items():
        noise = np.random.default_rng([zlib.crc32(name.encode()), seed]).standard_normal(out[name].shape)
        drawn = base * np.exp(spread * noise) if base else spread * noise
        out[name] = jnp.asarray(drawn.astype(out[name].dtype))
    for name, factor in factors.items():
        out[name] = (out[name] * factor).astype(out[name].dtype)
    return out
```

```python
def build_gnn_layer(nc, x, src, dst, edge_attr, w_left, b_left, w_right, b_right, out):
    from contextlib import ExitStack
    import concourse.bass as bass
    from concourse import mybir

    f32, i32, bf16 = mybir.dt.float32, mybir.dt.int32, mybir.dt.bfloat16
    ALU = mybir.AluOpType
    ACT = mybir.ActivationFunctionType

    P = 128
    N, D = x.shape
    E = src.shape[0]
    TILES = 4
    GE = TILES * P
    GROUPS = -(-E // GE)
    BLOCKS = -(-N // P)
    STEPS = GROUPS + BLOCKS - 1
    TAIL = E - (GROUPS - 1) * GE
    TAIL_P = TAIL // TILES
    ROWS_LAST = N - (BLOCKS - 1) * P
    SLOTS = 4
    BIG = 1.0e38
    SLOPE = 0.2
    EPS = 1.0e-5
    HP = GROUPS // 2
    HE = 2 * GE
    MW = GE + 2
    CH = 7
    SPARE = (BLOCKS - 1) * 2 * P + P - 1
    assert GROUPS % 2 == 0 and BLOCKS % CH == 0 and HP <= P and D == P and STEPS % SLOTS == 0
    assert TAIL % TILES == 0 and ROWS_LAST < P

    rows_dram = nc.dram_tensor("gather_rows", [BLOCKS * P, 2 * D], f32, kind="Internal").ap()
    field_dram = nc.dram_tensor("edge_fields", [GROUPS * P, 2 * TILES], i32, kind="Internal").ap()
    mask_dram = nc.dram_tensor("start_mask", [HP, 2 * MW], bf16, kind="Internal").ap()

    ctx = ExitStack()
    with ctx:
        def sb(name, shape, dt=f32):
            return ctx.enter_context(nc.sbuf_tensor(name, shape, dt))

        def pb(name):
            return ctx.enter_context(nc.psum_tensor(name, [P, 512], f32))

        def sem(name):
            return ctx.enter_context(nc.semaphore(name))

        right_all = sb("right_all", [P, BLOCKS, D])
        acc_all = sb("acc_all", [P, BLOCKS * 2 * P])
        acc_v = acc_all[:, :].rearrange("d (b c n) -> d b c n", b=BLOCKS, c=2)
        xh_all = acc_all[:, :].rearrange("p (b c) -> p b c", b=BLOCKS)

        field = sb("field", [P, SLOTS, 2 * TILES], i32)
        attr = sb("attr", [P, SLOTS, TILES * D])
        mask = sb("mask", [P, SLOTS, MW], bf16)
        xg = sb("xg", [P, SLOTS, TILES, 2 * D])
        gate = sb("gate", [P, SLOTS], i32)
        rel = sb("rel", [P, SLOTS, TILES])
        onehot = sb("onehot", [P, SLOTS, TILES, P])
        away = sb("away", [P, TILES, P])
        onehotT = sb("onehotT", [P, 2, TILES * P])
        v = sb("v", [P, TILES * D])
        s = sb("s", [P, TILES, D])
        F = sb("F", [P, 2, GE])
        B = sb("B", [P, GE])
        z = sb("z", [P, GE])
        eT = sb("eT", [P, GE])
        change = sb("change", [P, 2])
        factor = sb("factor", [P, 2])
        ex = sb("ex", [P, 2, 2, TILES, D])
        ident = sb("ident", [P, P])
        ones = sb("ones", [P, P])
        iota_i = sb("iota_i", [P, 256], i32)
        iota_f = sb("iota_f", [P, 256])
        iota_n = iota_f[:, 0:P]
        bias_row = sb("bias_row", [1, 2 * D])
        w_in = sb("w_in", [P, 2, D])
        wT = sb("wT", [P, 2 * D])
        xT = sb("xT", [P, 2, P])
        prev_dst = sb("prev_dst", [HP, 2], i32)
        prev_blk = sb("prev_blk", [HP, 2], i32)
        group_id = sb("group_id", [HP, 2], i32)
        first_step = sb("first_step", [HP, 2])
        prev_f = sb("prev_f", [HP, 2])
        blk_f = sb("blk_f", [HP, 2])
        gid_f = sb("gid_f", [HP, 2])
        goes_on = sb("goes_on", [HP, 2])
        column = sb("column", [HP, 2])
        group_f = sb("group_f", [P, STEPS])
        block_f = sb("block_f", [P, STEPS])
        work_f = sb("work_f", [1, 3, STEPS])
        node0 = sb("node0", [P, STEPS + SLOTS])
        tables = sb("tables", [1, 5, STEPS + SLOTS], i32)
        group_t, block_t, column_t, row_t, sums_t = (tables[0:1, i, :] for i in range(5))
        fields = sb("fields", [HP, HE // TILES, 2 * TILES], i32)
        dst_int = sb("dst_int", [HP, HE], i32)
        src_int = xg[0:HP, 0, :, :].rearrange("p i d -> p (i d)")[:, 0:HE].bitcast(i32)
        dst_f = xg[0:HP, 1, :, :].rearrange("p i d -> p (i d)")[:, 0:HE]
        differs = xg[0:HP, 2, :, :].rearrange("p i d -> p (i d)")[:, 0:HE]
        hits = onehot[0:HP, 0:2, :, :].rearrange("p c i n -> p c (i n)")
        marks = onehot[0:HP, 2:4, :, :].rearrange("p c i n -> p c (i n)")
        mask_prep = sb("mask_prep", [HP, 2, MW], bf16)
        stats = sb("stats", [P, CH, 6])
        mv = sb("mv", [P, CH, 2])
        std = sb("std", [P, CH])
        rstd = sb("rstd", [P, CH])
        eps = sb("eps", [P, 1])

        ps_ohT, ps_u, ps_sT, ps_e, ps_sum0, ps_sum1, ps_a, ps_b = (
            pb(n) for n in ("ps_ohT", "ps_u", "ps_sT", "ps_e", "ps_sum0", "ps_sum1", "ps_a", "ps_b"))
        ps_sum = [ps_sum0, ps_sum1]
        ps_x = [ps_ohT, ps_u]
        ps_left = [ps_sT, ps_e]
        ps_right = [ps_a, ps_b]

        c_set = sem("c_set"); c_iota = sem("c_iota"); c_id = sem("c_id")
        w_in_s = sem("w_in_s"); b_in_s = sem("b_in_s"); x_in = [sem(f"x_in{i}") for i in range(CH)]
        t_in = sem("t_in"); t_set = sem("t_set"); p_in = sem("p_in")
        wT_ps = sem("wT_ps"); wT_sb = sem("wT_sb")
        xT_ps = sem("xT_ps"); xT_sb = sem("xT_sb"); h_ps = sem("h_ps"); h_sb = sem("h_sb")
        r_sb = sem("r_sb")
        rows_out = sem("rows_out"); tables_out = sem("tables_out")
        dv = sem("dv")
        hits_ok = sem("hits_ok"); sched_ps = sem("sched_ps"); sched_ok = sem("sched_ok")
        tables_ok = sem("tables_ok"); acc_zero = sem("acc_zero")
        field_in = [sem(f"field_in{i}") for i in range(SLOTS)]
        attr_in = [sem(f"attr_in{i}") for i in range(SLOTS)]
        mask_in = [sem(f"mask_in{i}") for i in range(SLOTS)]
        rows_in = [sem(f"rows_in{i}") for i in range(SLOTS)]
        gate_ok = sem("gate_ok"); rel_ok = sem("rel_ok"); away_ok = sem("away_ok"); oh_ok = sem("oh_ok")
        ohT_ps = sem("ohT_ps"); ohT_sb = sem("ohT_sb")
        u_ps = sem("u_ps"); v_ok = sem("v_ok"); s_ok = sem("s_ok"); sT_ps = sem("sT_ps")
        F_ok = sem("F_ok"); B_ok = sem("B_ok"); z_ok = sem("z_ok"); change_ok = sem("change_ok")
        eT_ok = sem("eT_ok"); factor_ok = sem("factor_ok"); e_ps = sem("e_ps"); e_ok = sem("e_ok")
        msg_ok = sem("msg_ok"); sum_ps_ok = sem("sum_ps_ok"); scaled = sem("scaled"); acc_ok = sem("acc_ok")
        xf_in = [sem("xf_in0"), sem("xf_in1")]
        fin = sem("fin"); ratio_ok = sem("ratio_ok"); o_ps = sem("o_ps"); o_used = sem("o_used")
        y_ok = sem("y_ok"); var_ok = sem("var_ok"); std_ok = sem("std_ok")
        out_s = [sem("out_s0"), sem("out_s1")]

        xf = [xg[:, c, :, :].rearrange("p i d -> p (i d)")[:, 0:CH * D]
              .rearrange("p (b d) -> p b d", b=CH) for c in range(2)]

        def steps(body, eng, before, after):
            tail = STEPS - SLOTS
            for k in range(-before, SLOTS):
                body(k, k % SLOTS)
            with eng.Fori(SLOTS, tail, SLOTS) as k0:
                for j in range(SLOTS):
                    body(k0 + j, j)
            for k in range(tail, STEPS + after):
                body(k, k % SLOTS)

        def has(k):
            return not isinstance(k, int) or 0 <= k < STEPS

        def later(k, n):
            return not isinstance(k, int) or k >= n

        def turn(k, j, each):
            return each * (k // SLOTS if isinstance(k, int) else (k - j) // SLOTS) + each

        block = ctx.enter_context(nc.Block())

        @block.sync
        def _(sp):
            sp.dma_start(w_in[:, 0, :], w_left).then_inc(w_in_s, 16)
            sp.dma_start(w_in[:, 1, :], w_right).then_inc(w_in_s, 16)
            sp.dma_start(bias_row[0:1, 0:D], b_left.rearrange("(a n) -> a n", a=1)).then_inc(b_in_s, 16)
            sp.dma_start(bias_row[0:1, D:2 * D], b_right.rearrange("(a n) -> a n", a=1)).then_inc(b_in_s, 16)
            for c in range(CH):
                b0, b1 = c * CH, min((c + 1) * CH, BLOCKS - 1)
                if c == CH - 1:
                    sp.wait_ge(c_set, 1)
                    sp.dma_start(xh_all[0:ROWS_LAST, BLOCKS - 1, 0:D], x[(BLOCKS - 1) * P:N, :])\
                        .then_inc(x_in[c], 16)
                sp.dma_start(xh_all[:, b0:b1, 0:D],
                             x[b0 * P:b1 * P, :].rearrange("(b p) d -> p b d", p=P)).then_inc(x_in[c], 16)
            for c in range(CH):
                sp.wait_ge(h_sb, CH * (c + 1))
                sp.dma_start(rows_dram[c * CH * P:(c + 1) * CH * P, :].rearrange("(b p) d -> p b d", p=P),
                             xh_all[:, c * CH:(c + 1) * CH, :]).then_inc(rows_out, 16)
            sp.wait_ge(tables_out, 32)
            sp.wait_ge(sched_ok, 1)

            def fields_of(k, j):
                g = sp.value_load(group_t[:, bass.ds(k, 1)], min_val=0, max_val=GROUPS - 1)
                sp.dma_start(field[:, j, :], field_dram[bass.ds(g * P, P), :]).then_inc(field_in[j], 16)

            def loads(k, j):
                if has(k + 2):
                    jn = (j + 2) % SLOTS
                    if later(k, 2):
                        sp.wait_ge(oh_ok, k - 1)
                        sp.wait_ge(gate_ok, k - 1)
                        sp.wait_ge(rows_in[jn], turn(k - 2, jn, 64))
                    fields_of(k + 2, jn)
                if not has(k):
                    return
                g = sp.value_load(group_t[:, bass.ds(k, 1)], min_val=0, max_val=GROUPS - 1)
                r = sp.value_load(row_t[:, bass.ds(k, 1)], min_val=0, max_val=E - (GE - TAIL))
                if later(k, SLOTS):
                    sp.wait_ge(v_ok, k - SLOTS + 1)
                sp.dma_start(attr[0:TAIL_P, j, :],
                             edge_attr[bass.ds(g * GE, TAIL), :].rearrange("(p i) d -> p (i d)", i=TILES))\
                    .then_inc(attr_in[j], 16)
                sp.dma_start(attr[TAIL_P:P, j, :],
                             edge_attr[bass.ds(r, GE - TAIL), :].rearrange("(p i) d -> p (i d)", i=TILES))\
                    .then_inc(attr_in[j], 16)
                if later(k, SLOTS):
                    sp.wait_ge(B_ok, k - SLOTS + 1)
                m = mask_dram.rearrange("p (h e) -> (p h) e", h=2)[bass.ds(g, 1), :]
                sp.dma_start(mask[:, j, :], m.broadcast_to([P, MW])).then_inc(mask_in[j], 16)

            steps(loads, sp, 2, 0)

            sp.wait_ge(msg_ok, STEPS)
            for c in range(CH):
                b0, b1 = c * CH, min((c + 1) * CH, BLOCKS - 1)
                if c >= 2:
                    sp.wait_ge(out_s[c % 2], 16 * (c // 2))
                if c == CH - 1:
                    sp.dma_start(xf[c % 2][0:ROWS_LAST, CH - 1, :], x[(BLOCKS - 1) * P:N, :])\
                        .then_inc(xf_in[c % 2], 16)
                sp.dma_start(xf[c % 2][:, 0:b1 - b0, :],
                             x[b0 * P:b1 * P, :].rearrange("(b p) d -> p b d", p=P)).then_inc(xf_in[c % 2], 16)

        @block.gpsimd
        def _(pool):
            nc.gpsimd.memset(xh_all[:, BLOCKS - 1, :], 0.0).then_inc(c_set, 1)
            nc.gpsimd.memset(ident[:, :], 0.0).then_inc(c_id, 1)
            pool.wait_ge(c_id, 1)
            nc.gpsimd.affine_select(out=ident[:, :], in_=ident[:, :], compare_op=ALU.not_equal, fill=1.0,
                                    base=0, pattern=[[-1, P]], channel_multiplier=1).then_inc(c_id, 1)
            nc.gpsimd.memset(ones[:, :], 1.0).then_inc(c_id, 1)
            nc.gpsimd.iota(iota_i[:, :], [[1, 256]], base=0, channel_multiplier=0).then_inc(c_iota, 1)
            nc.gpsimd.iota(group_id[:, :], [[1, 2]], base=0, channel_multiplier=2).then_inc(c_iota, 1)
            pool.wait_ge(t_set, 3)
            whole = (HP - 1) * HE
            for t, a in ((dst_int[:, :], dst), (src_int, src)):
                pool.dma_start(t[0:HP - 1, :], a[0:whole].rearrange("(p e) -> p e", e=HE)).then_inc(t_in, 16)
                pool.dma_start(t[HP - 1:HP, 0:E - whole],
                               a[whole:E].rearrange("(a e) -> a e", a=1)).then_inc(t_in, 16)
            pool.dma_start(prev_dst[1:HP, 0:1], dst[0:whole].rearrange("(p e) -> p e", e=HE)[:, HE - 1:HE],
                           allow_slow_non_contiguous=True).then_inc(p_in, 16)
            pool.wait_ge(rows_out, 16 * CH)
            nc.gpsimd.memset(acc_all[:, :], 0.0).then_inc(acc_zero, 1)

            def gathers(k, j):
                if not has(k):
                    return
                pool.wait_ge(field_in[j], turn(k, j, 16))
                if later(k, SLOTS):
                    pool.wait_ge(msg_ok, k - SLOTS + 1)
                nc.gpsimd.tensor_tensor(gate[:, j:j + 1], field[:, j, 0:1], field[:, j, 0:1], ALU.add)\
                    .then_inc(gate_ok, 1)
                for i in range(TILES):
                    pool.indirect_dma_start(
                        out=xg[:, j, i, :], out_offset=None, in_=rows_dram,
                        in_offset=bass.IndirectOffsetOnAxis(ap=field[:, j, i:i + 1], axis=0),
                    ).then_inc(rows_in[j], 16)

            steps(gathers, pool, 0, 0)

        @block.tensor
        def _(pe):
            pe.wait_ge(c_id, 3)
            pe.wait_ge(w_in_s, 32)
            for h in range(2):
                nc.tensor.transpose(ps_a[:, h * D:(h + 1) * D], w_in[:, h, :], ident[:, :]).then_inc(wT_ps, 1)
            pe.wait_ge(wT_sb, 1)
            pe.wait_ge(b_in_s, 32)

            def flip(b):
                if b % CH == 0:
                    pe.wait_ge(x_in[b // CH], 16 + 16 * (b // CH == CH - 1))
                if b >= 2:
                    pe.wait_ge(xT_sb, b - 1)
                nc.tensor.transpose(ps_x[b % 2][:, 0:P], xh_all[:, b, 0:D], ident[:, :]).then_inc(xT_ps, 1)

            flip(0)
            for b in range(BLOCKS):
                if b + 1 < BLOCKS:
                    flip(b + 1)
                pe.wait_ge(xT_sb, b + 1)
                if b >= 2:
                    pe.wait_ge(h_sb, b - 1)
                    pe.wait_ge(r_sb, b - 1)
                for h, bank in ((0, ps_left), (1, ps_right)):
                    half = slice(h * D, (h + 1) * D)
                    nc.tensor.matmul(bank[b % 2][:, 0:D], ones[0:1, :], bias_row[0:1, half], start=True, stop=False)
                    last = nc.tensor.matmul(bank[b % 2][:, 0:D], xT[:, b % 2, :], wT[:, half], start=False, stop=True)
                last.then_inc(h_ps, 1)
            pe.wait_ge(hits_ok, 4)
            for c in range(2):
                nc.tensor.matmul(ps_sum0[:, 0:STEPS], ones[0:HP, :], hits[:, c, 0:STEPS],
                                 start=(c == 0), stop=(c == 1))
            for c in range(2):
                last = nc.tensor.matmul(ps_sum1[:, 0:STEPS], ones[0:HP, :], marks[:, c, 0:STEPS],
                                        start=(c == 0), stop=(c == 1))
            last.then_inc(sched_ps, 1)
            pe.wait_ge(h_sb, BLOCKS)
            pe.wait_ge(r_sb, BLOCKS)
            pe.wait_ge(sched_ok, 1)

            sT_view = ps_sT[:, :].rearrange("d (p i) -> d i p", i=TILES)
            eT_view = eT[:, :].rearrange("d (p i) -> d i p", i=TILES)

            def body(k, j):
                jp, jn, j2 = (j - 1) % SLOTS, (j + 1) % SLOTS, (j + 2) % SLOTS
                if has(k):
                    pe.wait_ge(s_ok, k + 1)
                    for i in range(TILES):
                        last = nc.tensor.transpose(sT_view[:, i, :], s[:, i, :], ident[:, :])
                    last.then_inc(sT_ps, 1)
                if has(k + 1):
                    pe.wait_ge(rows_in[jn], turn(k + 1, jn, 64))
                    nc.tensor.matmul(ps_u[:, :], ident[:, :], xg[:, jn, :, D:2 * D], start=True, stop=False)
                    b = pe.value_load(block_t[:, bass.ds(k + 1, 1)], min_val=0, max_val=BLOCKS - 1)
                    pe.wait_ge(ohT_sb, k + 2)
                    for i in range(TILES):
                        last = nc.tensor.matmul(ps_u[:, i * D:(i + 1) * D], onehotT[:, jn % 2, i * P:(i + 1) * P],
                                                right_all[:, bass.ds(b, 1), :].rearrange("p a d -> p (a d)"),
                                                start=False, stop=(i == TILES - 1))
                    last.then_inc(u_ps, 1)
                if has(k - 1):
                    pe.wait_ge(msg_ok, k)
                    if later(k, 3):
                        pe.wait_ge(acc_ok, k - 2)
                    for c in range(2):
                        for i in range(TILES):
                            last = nc.tensor.matmul(ps_sum[jp % 2][:, c * P:(c + 1) * P], ex[:, jp % 2, c, i, :],
                                                    onehot[:, jp, i, :], start=(i == 0), stop=(i == TILES - 1))
                    last.then_inc(sum_ps_ok, 1)
                if has(k):
                    pe.wait_ge(eT_ok, k + 1)
                    for i in range(TILES):
                        last = nc.tensor.transpose(ps_e[:, i * D:(i + 1) * D], eT_view[:, i, :], ident[:, :])
                    last.then_inc(e_ps, 1)
                if has(k + 2):
                    pe.wait_ge(oh_ok, k + 3)
                    for i in range(TILES):
                        last = nc.tensor.transpose(ps_ohT[:, i * P:(i + 1) * P], onehot[:, j2, i, :], ident[:, :])
                    last.then_inc(ohT_ps, 1)

            steps(body, pe, 2, 1)

            for b in range(BLOCKS):
                if b % CH == 0:
                    pe.wait_ge(ratio_ok, b // CH + 1)
                half, at = divmod(b % CH, 4)
                bank = (ps_a, ps_b)[half]
                if b >= CH and at == 0:
                    pe.wait_ge(o_used, b // CH)
                last = nc.tensor.transpose(bank[:, at * P:(at + 1) * P], acc_v[:, b, 1, :], ident[:, :])
                if b % CH == CH - 1:
                    last.then_inc(o_ps, 1)

        @block.scalar
        def _(act):
            act.wait_ge(wT_ps, 2)
            nc.scalar.activation(wT[:, :], ps_a[:, 0:2 * D], ACT.Copy).then_inc(wT_sb, 1)
            for b in range(BLOCKS):
                act.wait_ge(h_ps, b + 1)
                nc.scalar.activation(xh_all[:, b, D:2 * D], ps_left[b % 2][:, 0:D], ACT.Copy).then_inc(h_sb, 1)
            act.wait_ge(tables_ok, 1)
            act.dma_start(field_dram.rearrange("(p r) f -> p r f", p=HP), fields[:, :, :]).then_inc(tables_out, 16)
            act.dma_start(mask_dram, mask_prep[:, :, :].rearrange("p h e -> p (h e)")).then_inc(tables_out, 16)

            def body(k, j):
                j2 = (j + 2) % SLOTS
                if has(k + 2):
                    act.wait_ge(field_in[j2], turn(k + 2, j2, 16))
                    nc.scalar.activation(rel[:, j2, :], field[:, j2, TILES:2 * TILES].bitcast(f32), ACT.Identity,
                                         bias=node0[:, bass.ds(k + 2, 1)], scale=-1.0).then_inc(rel_ok, 1)
                    act.wait_ge(rel_ok, k + 3)
                    if later(k, 2):
                        act.wait_ge(sum_ps_ok, k - 1)
                    for i in range(TILES):
                        last = nc.scalar.activation(away[:, i, :], iota_n, ACT.Abs, bias=rel[:, j2, i:i + 1])
                    last.then_inc(away_ok, 1)
                    act.wait_ge(away_ok, k + 3)
                    nc.scalar.activation(onehot[:, j2, :, :], away[:, :, :], ACT.Relu, bias=ones[:, 0:1], scale=-1.0)                        .then_inc(oh_ok, 1)
                if has(k - 2):
                    c = act.value_load(column_t[:, bass.ds(k - 2, 1)], min_val=0, max_val=SPARE)
                    pair = acc_all[:, bass.ds(c, 2, P)]
                    if later(k, 3):
                        act.wait_ge(acc_ok, k - 2)
                    nc.scalar.activation(pair, pair, ACT.Copy, scale=factor[:, j % 2:j % 2 + 1]).then_inc(scaled, 1)
                if has(k):
                    act.wait_ge(z_ok, k + 1)
                    if later(k, 1):
                        act.wait_ge(e_ps, k)
                    nc.scalar.activation(eT[:, :], z[:, :], ACT.Exp).then_inc(eT_ok, 1)
                    act.wait_ge(change_ok, k + 1)
                    if later(k, 2):
                        act.wait_ge(scaled, k - 1)
                    nc.scalar.activation(factor[:, j % 2:j % 2 + 1], change[:, j % 2:j % 2 + 1], ACT.Exp)\
                        .then_inc(factor_ok, 1)
                    act.wait_ge(e_ps, k + 1)
                    if later(k, 2):
                        act.wait_ge(sum_ps_ok, k - 1)
                    nc.scalar.activation(ex[:, j % 2, 0, :, :].rearrange("p i d -> p (i d)"), ps_e[:, :], ACT.Copy)\
                        .then_inc(e_ok, 1)
                if has(k + 2):
                    act.wait_ge(ohT_ps, k + 3)
                    nc.scalar.activation(onehotT[:, j % 2, :], ps_ohT[:, :], ACT.Copy).then_inc(ohT_sb, 1)

            act.wait_ge(c_iota, 2)
            act.wait_ge(c_id, 3)
            act.wait_ge(sched_ok, 1)
            steps(body, act, 2, 2)

            for c in range(CH):
                act.wait_ge(var_ok, c + 1)
                nc.scalar.activation(std[:, :], mv[:, :, 1], ACT.Sqrt, bias=eps[:, 0:1]).then_inc(std_ok, 1)
                act.wait_ge(y_ok, c + 1)
                b0, b1 = c * CH, min((c + 1) * CH, BLOCKS - 1)
                if c == CH - 1:
                    act.dma_start(out[(BLOCKS - 1) * P:N, :], xf[c % 2][0:ROWS_LAST, CH - 1, :])\
                        .then_inc(out_s[c % 2], 16)
                act.dma_start(out[b0 * P:b1 * P, :].rearrange("(b p) d -> p b d", p=P),
                              xf[c % 2][:, 0:b1 - b0, :]).then_inc(out_s[c % 2], 16)
            act.wait_ge(out_s[0], 16 * 5)
            act.wait_ge(out_s[1], 16 * 3)

        @block.vector
        def _(dve):
            n_dv = [0]

            def chained(ins):
                n_dv[0] += 1
                ins.then_inc(dv, 1)
                dve.wait_ge(dv, n_dv[0])

            V = nc.vector
            V.memset(dst_int[:, :], -1).then_inc(t_set, 1)
            V.memset(src_int, 0).then_inc(t_set, 1)
            V.memset(prev_dst[:, :], 0).then_inc(t_set, 1)
            V.memset(eps[:, :], EPS)
            V.memset(F[:, 1, GE - 1:GE], -BIG)

            for b in range(BLOCKS):
                dve.wait_ge(xT_ps, b + 1)
                if b >= 2:
                    dve.wait_ge(h_ps, b - 1)
                V.tensor_copy(xT[:, b % 2, :], ps_x[b % 2][:, 0:P]).then_inc(xT_sb, 1)
                if b >= 1:
                    dve.wait_ge(h_ps, b)
                    V.tensor_copy(right_all[:, b - 1, :], ps_right[(b - 1) % 2][:, 0:D]).then_inc(r_sb, 1)
            dve.wait_ge(h_ps, BLOCKS)
            V.tensor_copy(right_all[:, BLOCKS - 1, :], ps_right[(BLOCKS - 1) % 2][:, 0:D]).then_inc(r_sb, 1)

            dve.wait_ge(t_in, 64)
            dve.wait_ge(p_in, 16)
            fv = fields[:, :, :].rearrange("p r (f i) -> p r f i", f=2)
            quad = lambda a: a.rearrange("p (r i) -> p r i", i=TILES)
            V.tensor_copy(fv[:, :, 0, :], quad(src_int))
            chained(V.tensor_copy(prev_dst[:, 1:2], dst_int[:, GE - 1:GE]))
            V.tensor_copy(prev_f[:, :], prev_dst[:, :])
            chained(V.tensor_copy(dst_f, dst_int[:, :]))
            V.tensor_copy(fv[:, :, 1, :].bitcast(f32), quad(dst_f))
            V.tensor_tensor(differs[:, 1:HE], dst_f[:, 0:HE - 1], dst_f[:, 1:HE], ALU.not_equal)
            chained(V.tensor_tensor(differs[:, 0:1], prev_f[:, 0:1], dst_f[:, 0:1], ALU.not_equal))
            V.memset(mask_prep[:, :, GE:MW], 0.0)
            V.tensor_scalar(mask_prep[:, :, 0:GE], differs.rearrange("p (h e) -> p h e", h=2), -BIG, None, ALU.mult)\
                .then_inc(tables_ok, 1)

            dve.wait_ge(c_iota, 2)
            V.tensor_copy(iota_f[:, :], iota_i[:, :])
            V.tensor_copy(gid_f[:, :], group_id[:, :])
            chained(V.tensor_scalar(prev_blk[:, :], prev_dst[:, :], 7, None, ALU.arith_shift_right))
            chained(V.tensor_copy(blk_f[:, :], prev_blk[:, :]))
            V.tensor_tensor(first_step[:, :], gid_f[:, :], blk_f[:, :], ALU.add)
            V.tensor_scalar(goes_on[:, :], differs.rearrange("p (h e) -> p h e", h=2)[:, :, 0], -1.0, 1.0,
                            ALU.mult, ALU.add)
            chained(V.scalar_tensor_tensor(out=column[:, :], in0=blk_f[:, :], scalar=float(P), in1=prev_f[:, :],
                                           op0=ALU.mult, op1=ALU.add))
            chained(V.scalar_tensor_tensor(out=column[:, :], in0=column[:, :], scalar=-float(SPARE),
                                           in1=goes_on[:, :], op0=ALU.add, op1=ALU.mult))
            for c in range(2):
                V.tensor_scalar(hits[:, c, 0:STEPS], iota_f[0:HP, 0:STEPS], first_step[:, c:c + 1], None,
                                ALU.is_ge).then_inc(hits_ok, 1)
                V.tensor_scalar(marks[:, c, 0:STEPS], iota_f[0:HP, 0:STEPS], first_step[:, c:c + 1],
                                column[:, c:c + 1], ALU.is_equal, ALU.mult).then_inc(hits_ok, 1)
            dve.wait_ge(sched_ps, 1)
            chained(V.tensor_scalar(group_f[:, :], ps_sum0[:, 0:STEPS], -1.0, None, ALU.add))
            V.tensor_scalar(work_f[:, 0, :], group_f[0:1, :], float(GE), float(TAIL), ALU.mult, ALU.add)
            V.tensor_scalar(work_f[:, 1, :], ps_sum1[0:1, 0:STEPS], float(SPARE), None, ALU.add)
            chained(V.tensor_tensor(block_f[:, :], iota_f[:, 0:STEPS], group_f[:, :], ALU.subtract))
            V.tensor_scalar(node0[:, 0:STEPS], block_f[:, :], float(P), None, ALU.mult)
            V.tensor_copy(group_t[:, 0:STEPS], group_f[0:1, :])
            V.tensor_copy(block_t[:, 0:STEPS], block_f[0:1, :])
            V.tensor_scalar(sums_t[:, 0:STEPS], block_f[0:1, :], float(2 * P), None, ALU.mult)
            V.tensor_copy(column_t[:, 0:STEPS], work_f[:, 1, :])
            chained(V.tensor_scalar(work_f[:, 2, :], work_f[:, 0, :], float(E - (GE - TAIL)), None, ALU.min))
            chained(V.tensor_copy(row_t[:, 0:STEPS], work_f[:, 2, :]))
            V.memset(change[:, :], 0.0).then_inc(sched_ok, 1)
            dve.wait_ge(acc_zero, 1)
            dve.wait_ge(sched_ok, 1)

            def body(k, j):
                jp = (j - 1) % SLOTS
                now, prev, before = has(k), has(k - 1), has(k - 2)
                if now:
                    dve.wait_ge(attr_in[j], turn(k, j, 32))
                    dve.wait_ge(u_ps, k + 1)
                    V.tensor_tensor(v[:, :], ps_u[:, :], attr[:, j, :], ALU.mult).then_inc(v_ok, 1)
                if now:
                    dve.wait_ge(v_ok, k + 1)
                    V.scalar_tensor_tensor(out=s[:, :, :].rearrange("p i d -> p (i d)"), in0=v[:, :],
                                           scalar=SLOPE, in1=v[:, :], op0=ALU.mult, op1=ALU.max).then_inc(s_ok, 1)
                if prev:
                    dve.wait_ge(e_ok, k)
                    V.tensor_tensor(ex[:, jp % 2, 1, :, :], ex[:, jp % 2, 0, :, :], xg[:, jp, :, 0:D], ALU.mult)                        .then_inc(msg_ok, 1)
                if now:
                    dve.wait_ge(mask_in[j], turn(k, j, 16))
                    dve.wait_ge(sT_ps, k + 1)
                    V.tensor_tensor_scan(F[:, j % 2, :], mask[:, j, 0:GE], ps_sT[:, :],
                                         F[:, (j - 1) % 2, GE - 1:GE], ALU.add, ALU.max).then_inc(F_ok, 1)
                if before:
                    at = dve.value_load(sums_t[:, bass.ds(k - 2, 1)], min_val=0, max_val=(BLOCKS - 1) * 2 * P)
                    sums = acc_all[:, bass.ds(at, 2 * P)]
                if now:
                    dve.wait_ge(F_ok, k + 1)
                    V.tensor_tensor_scan(B[:, ::-1], mask[:, j, GE:0:-1], F[:, j % 2, ::-1], -BIG,
                                         ALU.add, ALU.max).then_inc(B_ok, 1)
                    dve.wait_ge(B_ok, k + 1)
                    V.tensor_scalar(change[:, j % 2:j % 2 + 1], F[:, (j - 1) % 2, GE - 1:GE], B[:, 0:1], 0.0,
                                    ALU.subtract, ALU.min).then_inc(change_ok, 1)
                    V.tensor_tensor(z[:, :], ps_sT[:, :], B[:, :], ALU.subtract).then_inc(z_ok, 1)
                if before:
                    dve.wait_ge(scaled, k - 1)
                    dve.wait_ge(sum_ps_ok, k - 1)
                    V.tensor_tensor(sums, sums, ps_sum[j % 2][:, 0:2 * P], ALU.add).then_inc(acc_ok, 1)

            steps(body, dve, 2, 2)

            n_fin = [0]

            def done(ins):
                n_fin[0] += 1
                ins.then_inc(fin, 1)
                dve.wait_ge(fin, n_fin[0])

            dve.wait_ge(acc_ok, STEPS)

            def ratios(c):
                den, num = (acc_v[:, c * CH:(c + 1) * CH, i, :] for i in range(2))
                done(V.tensor_scalar(den, den, 1.0e-30, None, ALU.max))
                done(V.reciprocal(den, den))
                V.tensor_tensor(num, num, den, ALU.mult).then_inc(ratio_ok, 1)

            ratios(0)
            for c in range(CH):
                if c + 1 < CH:
                    ratios(c + 1)
                y = xf[c % 2]
                dve.wait_ge(xf_in[c % 2], 16 * (c // 2 + 1) + 16 * (c == CH - 1))
                dve.wait_ge(o_ps, c + 1)
                V.tensor_tensor(y[:, 0:4, :], y[:, 0:4, :], ps_a[:, :].rearrange("p (b d) -> p b d", d=D), ALU.add)
                V.tensor_tensor(y[:, 4:CH, :], y[:, 4:CH, :],
                                ps_b[:, 0:(CH - 4) * D].rearrange("p (b d) -> p b d", d=D), ALU.add)\
                    .then_inc(o_used, 1)
                dve.wait_ge(o_used, c + 1)
                for b in range(CH):
                    last = V.bn_stats(stats[:, b, :], y[:, b, :])
                done(last)
                for b in range(CH):
                    last = V.bn_aggr(mv[:, b, :], stats[:, b, :])
                last.then_inc(var_ok, 1)
                dve.wait_ge(std_ok, c + 1)
                done(V.reciprocal(rstd[:, :], std[:, :]))
                for b in range(CH):
                    last = V.tensor_scalar(y[:, b, :], y[:, b, :], mv[:, b, 0:1], rstd[:, b:b + 1],
                                           ALU.subtract, ALU.mult)
                last.then_inc(y_ok, 1)


_OUTS = [((6250, 128), "float32")]


def kernel(x, src, dst, edge_attr_128, L0_gnn_Wl, L0_gnn_bl, L0_gnn_Wr, L0_gnn_br):
    import numpy as np
    import concourse.bacc as bacc
    from concourse import mybir
    from concourse.bass_utils import run_bass_kernel_spmd

    nc = bacc.Bacc("TRN2", target_bir_lowering=False, num_devices=1)
    given = {"x_in": x, "src_in": src, "dst_in": dst, "edge_attr_in": edge_attr_128, "w_left": L0_gnn_Wl,
             "b_left": L0_gnn_bl, "w_right": L0_gnn_Wr, "b_right": L0_gnn_br}
    arrays = {n: np.ascontiguousarray(a) for n, a in given.items()}
    args = [nc.dram_tensor(n, a.shape, mybir.dt.from_np(a.dtype), kind="ExternalInput").ap()
            for n, a in arrays.items()]
    out = nc.dram_tensor("out", (6250, 128), mybir.dt.float32, kind="ExternalOutput").ap()
    build_gnn_layer(nc, *args, out)
    r = run_bass_kernel_spmd(nc, [arrays], core_ids=[0])
    return r.results[0]["out"]
```

```python
def build_gnn_layer(nc, x, src, dst, edge_attr, w_left, b_left, w_right, b_right, out):
    from contextlib import ExitStack
    import concourse.bass as bass
    from concourse import mybir

    f32, i32, bf16 = mybir.dt.float32, mybir.dt.int32, mybir.dt.bfloat16
    f32r = mybir.dt.float32r
    ALU = mybir.AluOpType
    ACT = mybir.ActivationFunctionType

    P = 128
    N, D = x.shape
    E = src.shape[0]
    TILES = 4
    GE = TILES * P
    GROUPS = -(-E // GE)
    BLOCKS = -(-N // P)
    STEPS = GROUPS + BLOCKS - 1
    TAIL = E - (GROUPS - 1) * GE
    TAIL_P = TAIL // TILES
    ROWS_LAST = N - (BLOCKS - 1) * P
    SLOTS = 6
    BIG = 1.0e38
    SLOPE = 0.2
    EPS = 1.0e-5
    HP = GROUPS // 2
    HE = 2 * GE
    MW = GE + 2
    EARLY_TURN = -(-(GROUPS + 2) // SLOTS)
    EARLY_EACH = 2
    EARLY_BLOCKS = len(range(EARLY_TURN * SLOTS, STEPS, SLOTS // EARLY_EACH))
    CH = 7
    QUAD = 4
    QUADS = -(-BLOCKS // QUAD)
    SCHED_QUAD = 9
    SPARE = (BLOCKS - 1) * 2 * P + P - 1
    assert GROUPS % 2 == 0 and BLOCKS % CH == 0 and HP <= P and D == P and SLOTS % 2 == 0
    assert TAIL % TILES == 0 and ROWS_LAST < P

    rows_dram = nc.dram_tensor("gather_rows", [BLOCKS * P, 2 * D], f32, kind="Internal").ap()
    field_dram = nc.dram_tensor("edge_fields", [GROUPS * P, 2 * TILES], i32, kind="Internal").ap()
    mask_dram = nc.dram_tensor("start_mask", [HP, 2 * MW], bf16, kind="Internal").ap()

    ctx = ExitStack()
    with ctx:
        def sb(name, shape, dt=f32):
            return ctx.enter_context(nc.sbuf_tensor(name, shape, dt))

        def pb(name, dt=f32):
            return ctx.enter_context(nc.psum_tensor(name, [P, 512], dt))

        def sem(name):
            return ctx.enter_context(nc.semaphore(name))

        right_all = sb("right_all", [P, BLOCKS, D])
        acc_all = sb("acc_all", [P, BLOCKS * 2 * P])
        acc_v = acc_all[:, :].rearrange("d (b c n) -> d b c n", b=BLOCKS, c=2)
        xh_all = acc_all[:, :].rearrange("p (b c) -> p b c", b=BLOCKS)

        field = sb("field", [P, SLOTS, 2 * TILES], i32)
        attr = sb("attr", [P, SLOTS, TILES * D])
        mask = sb("mask", [P, SLOTS, MW], bf16)
        xg = sb("xg", [P, SLOTS, TILES, 2 * D])
        gate = sb("gate", [P, SLOTS], i32)
        rel = sb("rel", [P, SLOTS, TILES])
        onehot = sb("onehot", [P, SLOTS, TILES, P], f32r)
        away = sb("away", [P, TILES, P])
        onehotT = sb("onehotT", [P, 2, TILES * P], f32r)
        v = sb("v", [P, TILES * D])
        s = sb("s", [P, 2, TILES, D])
        F = sb("F", [P, 2, GE])
        B = sb("B", [P, GE])
        z = sb("z", [P, GE])
        eT = sb("eT", [P, GE])
        change = sb("change", [P, 2])
        factor = sb("factor", [P, 2])
        ex = sb("ex", [P, 2, 2, TILES, D])
        ident = sb("ident", [P, P])
        ident_r = sb("ident_r", [P, P], f32r)
        ones = sb("ones", [P, P])
        iota_i = sb("iota_i", [P, 256], i32)
        iota_f = sb("iota_f", [P, 256])
        iota_n = iota_f[:, 0:P]
        bias = sb("bias", [P, 2, D])
        both = sb("both", [P, D])
        w_in = sb("w_in", [P, 2, D])
        wT = sb("wT", [P, 2 * D])
        xT = sb("xT", [P, 2, QUAD, P])
        prev_dst = sb("prev_dst", [HP, 2], i32)
        prev_blk = sb("prev_blk", [HP, 2], i32)
        group_id = sb("group_id", [HP, 2], i32)
        first_step = sb("first_step", [HP, 2])
        prev_f = sb("prev_f", [HP, 2])
        blk_f = sb("blk_f", [HP, 2])
        gid_f = sb("gid_f", [HP, 2])
        goes_on = sb("goes_on", [HP, 2])
        column = sb("column", [HP, 2])
        group_f = sb("group_f", [P, STEPS])
        block_f = sb("block_f", [P, STEPS])
        work_f = sb("work_f", [1, 3, STEPS])
        node0 = sb("node0", [P, STEPS + SLOTS])
        tables = sb("tables", [1, 5, STEPS + SLOTS], i32)
        group_t, block_t, column_t, row_t, sums_t = (tables[0:1, i, :] for i in range(5))
        fields = attr[0:HP, 0:4, :].rearrange("p s d -> p (s d)").bitcast(i32)\
            .rearrange("p (r f) -> p r f", f=2 * TILES)
        dst_int = attr[0:HP, 4:6, :].rearrange("p s d -> p (s d)").bitcast(i32)
        src_int = xg[0:HP, 0, :, :].rearrange("p i d -> p (i d)")[:, 0:HE].bitcast(i32)
        dst_f = xg[0:HP, 1, :, :].rearrange("p i d -> p (i d)")[:, 0:HE]
        differs = xg[0:HP, 2, :, :].rearrange("p i d -> p (i d)")[:, 0:HE]
        hits = F[0:HP, :, :]
        marks = s[0:HP, :, :, :].rearrange("p c i n -> p c (i n)")
        mask_prep = sb("mask_prep", [HP, 2, MW], bf16)
        stats = sb("stats", [P, CH, 6])
        mv = sb("mv", [P, 2, CH, 2])
        std = sb("std", [P, 2, CH])
        rstd = sb("rstd", [P, 2, CH])
        shift = sb("shift", [P, 2, CH])
        y = attr[:, 0:4, :].rearrange("p (c s) d -> p c (s d)", c=2)[:, :, 0:CH * D]\
            .rearrange("p c (b d) -> p c b d", b=CH)
        eps = sb("eps", [P, 1])

        ps_ohT = pb("ps_ohT", f32r)
        ps_e, ps_sum0, ps_sum1, ps_u0, ps_u1, ps_sT0, ps_sT1 = (
            pb(n) for n in ("ps_e", "ps_sum0", "ps_sum1", "ps_u0", "ps_u1", "ps_sT0", "ps_sT1"))
        ps_sum = [ps_sum0, ps_sum1]
        ps_u = [ps_u0, ps_u1]
        ps_sT = [ps_sT0, ps_sT1]
        ps_x = [ps_sum0, ps_sum1]
        ps_left = [ps_e, ps_u0]
        ps_right = [ps_u1, ps_sT0]
        ps_sched, ps_w = ps_sT1, ps_sT1
        ps_y = [(ps_e, ps_u0), (ps_u1, ps_sT0), (ps_sT1, ps_sum0)]

        c_set = sem("c_set"); c_iota = sem("c_iota"); c_id = sem("c_id"); identr_ok = sem("identr_ok")
        w_in_s = sem("w_in_s"); b_in_s = sem("b_in_s"); x_in = [sem(f"x_in{i}") for i in range(CH)]
        t_in = sem("t_in"); t_set = sem("t_set"); p_in = sem("p_in")
        wT_ps = sem("wT_ps"); wT_sb = sem("wT_sb")
        xT_ps = sem("xT_ps"); xT_sb = sem("xT_sb"); h_ps = sem("h_ps"); h_sb = sem("h_sb")
        r_sb = sem("r_sb")
        rows_out = [sem(f"rows_out{i}") for i in range(CH)]; both_ok = sem("both_ok"); tables_out = sem("tables_out")
        dv = sem("dv")
        hits_ok = sem("hits_ok"); sched_ps = sem("sched_ps"); sched_ok = sem("sched_ok")
        tables_ok = sem("tables_ok"); acc_zero = sem("acc_zero")
        field_in = [sem(f"field_in{i}") for i in range(SLOTS)]
        attr_in = [sem(f"attr_in{i}") for i in range(SLOTS)]
        mask_in = [sem(f"mask_in{i}") for i in range(SLOTS)]
        rows_in = [sem(f"rows_in{i}") for i in range(SLOTS)]
        gate_ok = sem("gate_ok"); rel_ok = sem("rel_ok"); away_ok = sem("away_ok"); oh_ok = sem("oh_ok")
        ohT_ps = sem("ohT_ps"); ohT_sb = sem("ohT_sb")
        u_ps = sem("u_ps"); v_ok = sem("v_ok"); s_ok = sem("s_ok"); sT_ps = sem("sT_ps")
        F_ok = sem("F_ok"); B_ok = sem("B_ok"); z_ok = sem("z_ok"); change_ok = sem("change_ok")
        eT_ok = sem("eT_ok"); factor_ok = sem("factor_ok"); e_ps = sem("e_ps"); e_ok = sem("e_ok")
        msg_ok = sem("msg_ok"); sum_ps_ok = sem("sum_ps_ok"); scaled = sem("scaled"); acc_ok = sem("acc_ok")
        xf_in = [sem("xf_in0"), sem("xf_in1")]
        fin = sem("fin"); early_ok = sem("early_ok"); recip_ok = sem("recip_ok"); ratio_ok = sem("ratio_ok"); o_ps = sem("o_ps"); shift_ok = sem("shift_ok")
        y_ok = sem("y_ok"); var_ok = sem("var_ok"); std_ok = sem("std_ok")
        out_s = [sem("out_s0"), sem("out_s1")]

        xf = [xg[:, c, :, :].rearrange("p i d -> p (i d)")[:, 0:CH * D]
              .rearrange("p (b d) -> p b d", b=CH) for c in range(2)]

        TURNS = STEPS // SLOTS - 1

        def steps(body, eng, before, after, early=None):
            for k in range(-before, SLOTS):
                body(k, k // SLOTS, k % SLOTS)
            for first, last, more in ((1, EARLY_TURN, None), (EARLY_TURN, TURNS, early)) if early else ((1, TURNS, None),):
                with eng.Fori(first, last) as t:
                    for j in range(SLOTS):
                        body(t * SLOTS + j, t, j)
                        if more:
                            more(t, j)
            for k in range(TURNS * SLOTS, STEPS + after):
                body(k, k // SLOTS, k % SLOTS)
                if early and k < STEPS:
                    early(k // SLOTS, k % SLOTS)

        def has(k):
            return not isinstance(k, int) or 0 <= k < STEPS

        def later(k, n):
            return not isinstance(k, int) or k >= n

        def turn(t, j, each):
            return (t + j // SLOTS) * each + each

        def empty(eng, c):
            eng.memset(acc_v[:, c * CH:(c + 1) * CH, 0, :], 1.0e-30)
            eng.memset(acc_v[:, c * CH:(c + 1) * CH, 1, :], 0.0).then_inc(acc_zero, 1)

        block = ctx.enter_context(nc.Block())

        @block.sync
        def _(sp):
            sp.dma_start(w_in[:, 0, :], w_left).then_inc(w_in_s, 16)
            sp.dma_start(w_in[:, 1, :], w_right).then_inc(w_in_s, 16)
            for h, b_in in ((0, b_left), (1, b_right)):
                sp.dma_start(bias[:, h, :], b_in.rearrange("(a n) -> a n", a=1).broadcast_to([P, D]))\
                    .then_inc(b_in_s, 16)
            for c in range(CH):
                b0, b1 = c * CH, min((c + 1) * CH, BLOCKS - 1)
                if c == CH - 1:
                    sp.wait_ge(c_set, 1)
                    sp.dma_start(xh_all[0:ROWS_LAST, BLOCKS - 1, 0:D], x[(BLOCKS - 1) * P:N, :])\
                        .then_inc(x_in[c], 16)
                sp.dma_start(xh_all[:, b0:b1, 0:D],
                             x[b0 * P:b1 * P, :].rearrange("(b p) d -> p b d", p=P)).then_inc(x_in[c], 16)
            for c in range(CH):
                sp.wait_ge(h_sb, -(-CH * (c + 1) // QUAD))
                sp.dma_start(rows_dram[c * CH * P:(c + 1) * CH * P, :].rearrange("(b p) d -> p b d", p=P),
                             xh_all[:, c * CH:(c + 1) * CH, :]).then_inc(rows_out[c], 16)
            sp.wait_ge(tables_out, 32)
            sp.wait_ge(sched_ok, 1)

            def fields_of(k, j):
                g = sp.value_load(group_t[:, bass.ds(k, 1)], min_val=0, max_val=GROUPS - 1)
                sp.dma_start(field[:, j, :], field_dram[bass.ds(g * P, P), :]).then_inc(field_in[j], 16)

            def loads(k, t, j):
                if has(k + 2):
                    jn = (j + 2) % SLOTS
                    if later(k + 2, SLOTS):
                        sp.wait_ge(oh_ok, k + 3 - SLOTS)
                        sp.wait_ge(gate_ok, k + 3 - SLOTS)
                        sp.wait_ge(rows_in[jn], turn(t, j + 2 - SLOTS, 64))
                    fields_of(k + 2, jn)
                if not has(k):
                    return
                g = sp.value_load(group_t[:, bass.ds(k, 1)], min_val=0, max_val=GROUPS - 1)
                r = sp.value_load(row_t[:, bass.ds(k, 1)], min_val=0, max_val=E - (GE - TAIL))
                if later(k, SLOTS):
                    sp.wait_ge(v_ok, k - SLOTS + 1)
                sp.dma_start(attr[0:TAIL_P, j, :],
                             edge_attr[bass.ds(g * GE, TAIL), :].rearrange("(p i) d -> p (i d)", i=TILES))\
                    .then_inc(attr_in[j], 16)
                sp.dma_start(attr[TAIL_P:P, j, :],
                             edge_attr[bass.ds(r, GE - TAIL), :].rearrange("(p i) d -> p (i d)", i=TILES))\
                    .then_inc(attr_in[j], 16)
                if later(k, SLOTS):
                    sp.wait_ge(B_ok, k - SLOTS + 1)
                m = mask_dram.rearrange("p (h e) -> (p h) e", h=2)[bass.ds(g, 1), :]
                sp.dma_start(mask[:, j, :], m.broadcast_to([P, MW])).then_inc(mask_in[j], 16)

            steps(loads, sp, 2, 0)

            sp.wait_ge(msg_ok, STEPS)
            for c in range(CH):
                b0, b1 = c * CH, min((c + 1) * CH, BLOCKS - 1)
                if c >= 2:
                    sp.wait_ge(o_ps, c - 1)
                if c == CH - 1:
                    sp.dma_start(xf[c % 2][0:ROWS_LAST, CH - 1, :], x[(BLOCKS - 1) * P:N, :])\
                        .then_inc(xf_in[c % 2], 16)
                sp.dma_start(xf[c % 2][:, 0:b1 - b0, :],
                             x[b0 * P:b1 * P, :].rearrange("(b p) d -> p b d", p=P)).then_inc(xf_in[c % 2], 16)

        @block.gpsimd
        def _(pool):
            nc.gpsimd.memset(xh_all[:, BLOCKS - 1, :], 0.0).then_inc(c_set, 1)
            nc.gpsimd.memset(ident[:, :], 0.0).then_inc(c_id, 1)
            pool.wait_ge(c_id, 1)
            nc.gpsimd.affine_select(out=ident[:, :], in_=ident[:, :], compare_op=ALU.not_equal, fill=1.0,
                                    base=0, pattern=[[-1, P]], channel_multiplier=1).then_inc(c_id, 1)
            nc.gpsimd.memset(ones[:, :], 1.0).then_inc(c_id, 1)
            nc.gpsimd.iota(iota_i[:, :], [[1, 256]], base=0, channel_multiplier=0).then_inc(c_iota, 1)
            nc.gpsimd.iota(group_id[:, :], [[1, 2]], base=0, channel_multiplier=2).then_inc(c_iota, 1)
            pool.wait_ge(t_set, 3)
            whole = (HP - 1) * HE
            for t, a in ((dst_int[:, :], dst), (src_int, src)):
                pool.dma_start(t[0:HP - 1, :], a[0:whole].rearrange("(p e) -> p e", e=HE)).then_inc(t_in, 16)
                pool.dma_start(t[HP - 1:HP, 0:E - whole],
                               a[whole:E].rearrange("(a e) -> a e", a=1)).then_inc(t_in, 16)
            pool.dma_start(prev_dst[1:HP, 0:1], dst[0:whole].rearrange("(p e) -> p e", e=HE)[:, HE - 1:HE],
                           allow_slow_non_contiguous=True).then_inc(p_in, 16)
            for c in range(CH):
                pool.wait_ge(rows_out[c], 16)
                if c < CH - 1:
                    empty(nc.gpsimd, c)

            def gathers(k, t, j):
                if not has(k):
                    return
                pool.wait_ge(field_in[j], turn(t, j, 16))
                if later(k, SLOTS):
                    pool.wait_ge(msg_ok, k - SLOTS + 1)
                nc.gpsimd.tensor_tensor(gate[:, j:j + 1], field[:, j, 0:1], field[:, j, 0:1], ALU.add)\
                    .then_inc(gate_ok, 1)
                for i in range(TILES):
                    pool.indirect_dma_start(
                        out=xg[:, j, i, :], out_offset=None, in_=rows_dram,
                        in_offset=bass.IndirectOffsetOnAxis(ap=field[:, j, i:i + 1], axis=0),
                    ).then_inc(rows_in[j], 16)

            steps(gathers, pool, 0, 0)

            for c in range(CH):
                den, num = (acc_v[:, c * CH:(c + 1) * CH, i, :] for i in range(2))
                pool.wait_ge(acc_ok, GROUPS - 1 + (c + 1) * CH)
                pool.wait_ge(early_ok, min((c + 1) * CH, EARLY_BLOCKS))
                if (c + 1) * CH > EARLY_BLOCKS:
                    pool.wait_ge(recip_ok, c + 1 - EARLY_BLOCKS // CH)
                nc.gpsimd.tensor_tensor(num, num, den, ALU.mult).then_inc(ratio_ok, 1)

        @block.tensor
        def _(pe):
            pe.wait_ge(c_id, 3)
            pe.wait_ge(w_in_s, 32)
            for h in range(2):
                nc.tensor.transpose(ps_w[:, h * D:(h + 1) * D], w_in[:, h, :], ident[:, :]).then_inc(wT_ps, 1)

            def flip(q):
                blocks = range(q * QUAD, min((q + 1) * QUAD, BLOCKS))
                c = blocks[-1] // CH
                pe.wait_ge(x_in[c], 16 + 16 * (c == CH - 1))
                if q >= 2:
                    pe.wait_ge(xT_sb, q - 1)
                for b in blocks:
                    last = nc.tensor.transpose(ps_x[q % 2][:, (b % QUAD) * P:(b % QUAD + 1) * P],
                                               xh_all[:, b, 0:D], ident[:, :])
                last.then_inc(xT_ps, 1)

            def schedule():
                pe.wait_ge(hits_ok, 4)
                for h, table in ((0, hits), (1, marks)):
                    for c in range(2):
                        last = nc.tensor.matmul(ps_sched[:, h * 256:h * 256 + STEPS], ones[0:HP, :], table[:, c, 0:STEPS],
                                                start=(c == 0), stop=(c == 1))
                last.then_inc(sched_ps, 1)

            flip(0)
            pe.wait_ge(wT_sb, 1)
            for q in range(QUADS):
                if q == SCHED_QUAD:
                    schedule()
                if q + 1 < QUADS:
                    flip(q + 1)
                pe.wait_ge(xT_sb, q + 1)
                if q >= 2:
                    pe.wait_ge(h_sb, q - 1)
                    pe.wait_ge(r_sb, q - 1)
                for h, bank in ((0, ps_left), (1, ps_right)):
                    for i in range(min(QUAD, BLOCKS - q * QUAD)):
                        last = nc.tensor.matmul(bank[q % 2][:, i * D:(i + 1) * D], xT[:, q % 2, i, :],
                                                wT[:, h * D:(h + 1) * D], start=True, stop=True)
                last.then_inc(h_ps, 1)
            pe.wait_ge(h_sb, QUADS)
            pe.wait_ge(r_sb, QUADS)
            pe.wait_ge(sched_ok, 1)
            pe.wait_ge(identr_ok, 1)

            sT_view = [bank[:, :].rearrange("d (p i) -> d i p", i=TILES) for bank in ps_sT]
            eT_view = eT[:, :].rearrange("d (p i) -> d i p", i=TILES)

            def body(k, t, j):
                jb, j1, j2, j3 = ((j + n) % SLOTS for n in (-2, 1, 2, 3))
                if has(k + 2):
                    u = ps_u[j % 2]
                    if later(k, 0):
                        pe.wait_ge(v_ok, k + 1)
                    pe.wait_ge(rows_in[j2], turn(t, j + 2, 64))
                    nc.tensor.matmul(u[:, :], ident[:, :], xg[:, j2, :, D:2 * D], start=True, stop=False)
                    b = pe.value_load(block_t[:, bass.ds(k + 2, 1)], min_val=0, max_val=BLOCKS - 1)
                    pe.wait_ge(ohT_sb, k + 3)
                    for i in range(TILES):
                        last = nc.tensor.matmul(u[:, i * D:(i + 1) * D], onehotT[:, j % 2, i * P:(i + 1) * P].bitcast(f32),
                                                right_all[:, bass.ds(b, 1), :].rearrange("p a d -> p (a d)"),
                                                start=False, stop=(i == TILES - 1))
                    last.then_inc(u_ps, 1)
                if has(k - 2):
                    pe.wait_ge(msg_ok, k - 1)
                    if later(k, 4):
                        pe.wait_ge(acc_ok, k - 3)
                    for c in range(2):
                        for i in range(TILES):
                            last = nc.tensor.matmul(ps_sum[j % 2][:, c * P:(c + 1) * P], ex[:, j % 2, c, i, :],
                                                    onehot[:, jb, i, :].bitcast(f32), start=(i == 0), stop=(i == TILES - 1))
                    last.then_inc(sum_ps_ok, 1)
                if has(k + 1):
                    pe.wait_ge(s_ok, k + 2)
                    for i in range(TILES):
                        last = nc.tensor.transpose(sT_view[j1 % 2][:, i, :], s[:, j1 % 2, i, :], ident[:, :])
                    last.then_inc(sT_ps, 1)
                if has(k + 3):
                    pe.wait_ge(oh_ok, k + 4)
                    for i in range(TILES):
                        last = nc.tensor.transpose(ps_ohT[:, i * P:(i + 1) * P], onehot[:, j3, i, :], ident_r[:, :])
                    last.then_inc(ohT_ps, 1)
                if has(k):
                    pe.wait_ge(eT_ok, k + 1)
                    for i in range(TILES):
                        last = nc.tensor.transpose(ps_e[:, i * D:(i + 1) * D], eT_view[:, i, :], ident[:, :])
                    last.then_inc(e_ps, 1)

            steps(body, pe, 3, 2)

            for c in range(CH):
                pe.wait_ge(xf_in[c % 2], 16 * (c // 2 + 1) + 16 * (c == CH - 1))
                if c >= 3:
                    pe.wait_ge(y_ok, c - 2)
                for bank, b0, n in zip(ps_y[c % 3], (0, QUAD), (QUAD, CH - QUAD)):
                    nc.tensor.matmul(bank[:, 0:n * D], ident[:, :], xf[c % 2][:, b0:b0 + n, :], start=True, stop=False)
                    if b0 == 0:
                        pe.wait_ge(ratio_ok, c + 1)
                    for i in range(n):
                        last = nc.tensor.matmul(bank[:, i * D:(i + 1) * D], acc_v[:, c * CH + b0 + i, 1, :],
                                                ident[:, :], start=False, stop=(i == n - 1))
                last.then_inc(o_ps, 1)

        @block.scalar
        def _(act):
            act.wait_ge(wT_ps, 2)
            nc.scalar.activation(wT[:, :], ps_w[:, 0:2 * D], ACT.Copy).then_inc(wT_sb, 1)

            def turned(q):
                n = min(QUAD, BLOCKS - q * QUAD)
                act.wait_ge(xT_ps, q + 1)
                if q >= 2:
                    act.wait_ge(h_ps, q - 1)
                nc.scalar.activation(xT[:, q % 2, 0:n, :], ps_x[q % 2][:, 0:n * P].rearrange("p (i n) -> p i n", i=n),
                                     ACT.Copy).then_inc(xT_sb, 1)

            turned(0)
            for q in range(QUADS):
                if q + 1 < QUADS:
                    turned(q + 1)
                n = min(QUAD, BLOCKS - q * QUAD)
                act.wait_ge(h_ps, q + 1)
                nc.scalar.activation(xh_all[:, q * QUAD:q * QUAD + n, D:2 * D],
                                     ps_left[q % 2][:, 0:n * D].rearrange("p (i d) -> p i d", i=n),
                                     ACT.Copy).then_inc(h_sb, 1)
                if q == 6:
                    act.wait_ge(tables_ok, 1)
                    act.dma_start(field_dram.rearrange("(p r) f -> p r f", p=HP), fields[:, :, :]).then_inc(tables_out, 16)
                    act.dma_start(mask_dram, mask_prep[:, :, :].rearrange("p h e -> p (h e)")).then_inc(tables_out, 16)

            def body(k, t, j):
                j3 = (j + 3) % SLOTS
                if has(k - 1):
                    act.wait_ge(e_ps, k)
                    if later(k, 3):
                        act.wait_ge(sum_ps_ok, k - 2)
                    nc.scalar.activation(ex[:, (j + 1) % 2, 0, :, :].rearrange("p i d -> p (i d)"), ps_e[:, :],
                                         ACT.Copy).then_inc(e_ok, 1)
                if has(k + 3):
                    act.wait_ge(field_in[j3], turn(t, j + 3, 16))
                    nc.scalar.activation(rel[:, j3, :], field[:, j3, TILES:2 * TILES].bitcast(f32), ACT.Identity,
                                         bias=node0[:, bass.ds(k + 3, 1)], scale=-1.0).then_inc(rel_ok, 1)
                if has(k - 2):
                    c = act.value_load(column_t[:, bass.ds(k - 2, 1)], min_val=0, max_val=SPARE)
                    pair = acc_all[:, bass.ds(c, 2, P)]
                    if later(k, 3):
                        act.wait_ge(acc_ok, k - 2)
                    else:
                        act.wait_ge(acc_zero, CH)
                    nc.scalar.activation(pair, pair, ACT.Copy, scale=factor[:, j % 2:j % 2 + 1]).then_inc(scaled, 1)
                if has(k + 3):
                    act.wait_ge(rel_ok, k + 4)
                    for i in range(TILES):
                        last = nc.scalar.activation(away[:, i, :], iota_n, ACT.Abs, bias=rel[:, j3, i:i + 1])
                    last.then_inc(away_ok, 1)
                    act.wait_ge(away_ok, k + 4)
                    nc.scalar.activation(onehot[:, j3, :, :], away[:, :, :], ACT.Relu, bias=ones[:, 0:1], scale=-1.0)\
                        .then_inc(oh_ok, 1)
                if has(k):
                    act.wait_ge(z_ok, k + 1)
                    if later(k, 1):
                        act.wait_ge(e_ps, k)
                    nc.scalar.activation(eT[:, :], z[:, :], ACT.Exp).then_inc(eT_ok, 1)
                    act.wait_ge(change_ok, k + 1)
                    if later(k, 2):
                        act.wait_ge(scaled, k - 1)
                    nc.scalar.activation(factor[:, j % 2:j % 2 + 1], change[:, j % 2:j % 2 + 1], ACT.Exp)\
                        .then_inc(factor_ok, 1)
                if has(k + 3):
                    act.wait_ge(ohT_ps, k + 4)
                    nc.scalar.activation(onehotT[:, j3 % 2, :], ps_ohT[:, :], ACT.Copy).then_inc(ohT_sb, 1)

            act.wait_ge(c_iota, 2)
            act.wait_ge(c_id, 3)
            nc.scalar.activation(ident_r[:, :], ident[:, :], ACT.Copy).then_inc(identr_ok, 1)
            act.wait_ge(sched_ok, 1)
            steps(body, act, 3, 2)

            for c in range(CH):
                act.wait_ge(var_ok, c + 1)
                nc.scalar.activation(std[:, c % 2, :], mv[:, c % 2, :, 1], ACT.Sqrt, bias=eps[:, 0:1]).then_inc(std_ok, 1)
                act.wait_ge(shift_ok, c + 1)
                if c >= 2:
                    act.wait_ge(out_s[c % 2], 16 * (c // 2))
                for b in range(CH):
                    last = nc.scalar.activation(y[:, c % 2, b, :], ps_y[c % 3][b // QUAD][:, (b % QUAD) * D:(b % QUAD + 1) * D],
                                                ACT.Identity, bias=shift[:, c % 2, b:b + 1], scale=rstd[:, c % 2, b:b + 1])
                last.then_inc(y_ok, 1)
                act.wait_ge(y_ok, c + 1)
                b0, b1 = c * CH, min((c + 1) * CH, BLOCKS - 1)
                if c == CH - 1:
                    act.dma_start(out[(BLOCKS - 1) * P:N, :], y[0:ROWS_LAST, c % 2, CH - 1, :])\
                        .then_inc(out_s[c % 2], 16)
                act.dma_start(out[b0 * P:b1 * P, :].rearrange("(b p) d -> p b d", p=P),
                              y[:, c % 2, 0:b1 - b0, :]).then_inc(out_s[c % 2], 16)
            act.wait_ge(out_s[0], 16 * 5)
            act.wait_ge(out_s[1], 16 * 3)

        @block.vector
        def _(dve):
            n_dv = [0]

            def chained(ins):
                n_dv[0] += 1
                ins.then_inc(dv, 1)
                dve.wait_ge(dv, n_dv[0])

            V = nc.vector
            V.memset(dst_int[:, :], -1).then_inc(t_set, 1)
            V.memset(src_int, 0).then_inc(t_set, 1)
            V.memset(prev_dst[:, :], 0).then_inc(t_set, 1)
            V.memset(eps[:, :], EPS)
            V.memset(F[:, 1, GE - 1:GE], -BIG)

            dve.wait_ge(b_in_s, 32)
            V.tensor_tensor(both[:, :], bias[:, 0, :], bias[:, 1, :], ALU.add).then_inc(both_ok, 1)
            dve.wait_ge(both_ok, 1)

            def rights(q):
                n = min(QUAD, BLOCKS - q * QUAD)
                dve.wait_ge(h_ps, q + 1)
                V.tensor_tensor(right_all[:, q * QUAD:q * QUAD + n, :],
                                ps_right[q % 2][:, 0:n * D].rearrange("p (i d) -> p i d", i=n),
                                both[:, None, :].broadcast_to([P, n, D]), ALU.add).then_inc(r_sb, 1)

            for q in range(0, 3):
                rights(q)

            dve.wait_ge(t_in, 64)
            dve.wait_ge(p_in, 16)
            fv = fields[:, :, :].rearrange("p r (f i) -> p r f i", f=2)
            quad = lambda a: a.rearrange("p (r i) -> p r i", i=TILES)
            V.tensor_copy(fv[:, :, 0, :], quad(src_int))
            chained(V.tensor_copy(prev_dst[:, 1:2], dst_int[:, GE - 1:GE]))
            V.tensor_copy(prev_f[:, :], prev_dst[:, :])
            chained(V.tensor_copy(dst_f, dst_int[:, :]))
            V.tensor_copy(fv[:, :, 1, :].bitcast(f32), quad(dst_f))
            V.tensor_tensor(differs[:, 1:HE], dst_f[:, 0:HE - 1], dst_f[:, 1:HE], ALU.not_equal)
            chained(V.tensor_tensor(differs[:, 0:1], prev_f[:, 0:1], dst_f[:, 0:1], ALU.not_equal))
            V.memset(mask_prep[:, :, GE:MW], 0.0)
            V.tensor_scalar(mask_prep[:, :, 0:GE], differs.rearrange("p (h e) -> p h e", h=2), -BIG, None, ALU.mult)\
                .then_inc(tables_ok, 1)

            for q in range(3, 6):
                rights(q)

            dve.wait_ge(c_iota, 2)
            V.tensor_copy(iota_f[:, :], iota_i[:, :])
            V.tensor_copy(gid_f[:, :], group_id[:, :])
            chained(V.tensor_scalar(prev_blk[:, :], prev_dst[:, :], 7, None, ALU.arith_shift_right))
            chained(V.tensor_copy(blk_f[:, :], prev_blk[:, :]))
            V.tensor_tensor(first_step[:, :], gid_f[:, :], blk_f[:, :], ALU.add)
            V.tensor_scalar(goes_on[:, :], differs.rearrange("p (h e) -> p h e", h=2)[:, :, 0], -1.0, 1.0,
                            ALU.mult, ALU.add)
            chained(V.scalar_tensor_tensor(out=column[:, :], in0=blk_f[:, :], scalar=float(P), in1=prev_f[:, :],
                                           op0=ALU.mult, op1=ALU.add))
            chained(V.scalar_tensor_tensor(out=column[:, :], in0=column[:, :], scalar=-float(SPARE),
                                           in1=goes_on[:, :], op0=ALU.add, op1=ALU.mult))
            for c in range(2):
                V.tensor_scalar(hits[:, c, 0:STEPS], iota_f[0:HP, 0:STEPS], first_step[:, c:c + 1], None,
                                ALU.is_ge).then_inc(hits_ok, 1)
                V.tensor_scalar(marks[:, c, 0:STEPS], iota_f[0:HP, 0:STEPS], first_step[:, c:c + 1],
                                column[:, c:c + 1], ALU.is_equal, ALU.mult).then_inc(hits_ok, 1)

            for q in range(6, SCHED_QUAD + 1):
                rights(q)
            dve.wait_ge(sched_ps, 1)
            chained(V.tensor_scalar(group_f[:, :], ps_sched[:, 0:STEPS], -1.0, None, ALU.add))
            V.tensor_scalar(work_f[:, 0, :], group_f[0:1, :], float(GE), float(TAIL), ALU.mult, ALU.add)
            V.tensor_scalar(work_f[:, 1, :], ps_sched[0:1, 256:256 + STEPS], float(SPARE), None, ALU.add)
            chained(V.tensor_tensor(block_f[:, :], iota_f[:, 0:STEPS], group_f[:, :], ALU.subtract))
            V.tensor_scalar(node0[:, 0:STEPS], block_f[:, :], float(P), None, ALU.mult)
            V.tensor_copy(group_t[:, 0:STEPS], group_f[0:1, :])
            V.tensor_copy(block_t[:, 0:STEPS], block_f[0:1, :])
            V.tensor_scalar(sums_t[:, 0:STEPS], block_f[0:1, :], float(2 * P), None, ALU.mult)
            V.tensor_copy(column_t[:, 0:STEPS], work_f[:, 1, :])
            chained(V.tensor_scalar(work_f[:, 2, :], work_f[:, 0, :], float(E - (GE - TAIL)), None, ALU.min))
            chained(V.tensor_copy(row_t[:, 0:STEPS], work_f[:, 2, :]))
            V.memset(change[:, :], 0.0).then_inc(sched_ok, 1)

            for q in range(SCHED_QUAD + 1, QUADS):
                rights(q)

            dve.wait_ge(rows_out[CH - 1], 16)
            empty(V, CH - 1)
            dve.wait_ge(acc_zero, CH)
            dve.wait_ge(sched_ok, 1)

            def body(k, t, j):
                j1, jp = (j + 1) % SLOTS, (j - 1) % SLOTS
                if has(k + 1):
                    if later(k, 0):
                        dve.wait_ge(s_ok, k + 1)
                    dve.wait_ge(attr_in[j1], turn(t, j + 1, 32))
                    dve.wait_ge(u_ps, k + 2)
                    V.tensor_tensor(v[:, :], ps_u[j1 % 2][:, :], attr[:, j1, :], ALU.mult).then_inc(v_ok, 1)
                    dve.wait_ge(v_ok, k + 2)
                    V.scalar_tensor_tensor(out=s[:, j1 % 2, :, :].rearrange("p i d -> p (i d)"), in0=v[:, :],
                                           scalar=SLOPE, in1=v[:, :], op0=ALU.mult, op1=ALU.max).then_inc(s_ok, 1)
                if has(k):
                    dve.wait_ge(mask_in[j], turn(t, j, 16))
                    dve.wait_ge(sT_ps, k + 1)
                    if later(k, 1):
                        dve.wait_ge(change_ok, k)
                    V.tensor_tensor_scan(F[:, j % 2, :], mask[:, j, 0:GE], ps_sT[j % 2][:, :],
                                         F[:, (j - 1) % 2, GE - 1:GE], ALU.add, ALU.max).then_inc(F_ok, 1)
                if has(k - 2):
                    at = dve.value_load(sums_t[:, bass.ds(k - 2, 1)], min_val=0, max_val=(BLOCKS - 1) * 2 * P)
                    sums = acc_all[:, bass.ds(at, 2 * P)]
                if has(k):
                    dve.wait_ge(F_ok, k + 1)
                    V.tensor_tensor_scan(B[:, ::-1], mask[:, j, GE:0:-1], F[:, j % 2, ::-1], -BIG,
                                         ALU.add, ALU.max).then_inc(B_ok, 1)
                    dve.wait_ge(B_ok, k + 1)
                    V.tensor_scalar(change[:, j % 2:j % 2 + 1], F[:, (j - 1) % 2, GE - 1:GE], B[:, 0:1], 0.0,
                                    ALU.subtract, ALU.min).then_inc(change_ok, 1)
                    if later(k, 1):
                        dve.wait_ge(eT_ok, k)
                    V.tensor_tensor(z[:, :], ps_sT[j % 2][:, :], B[:, :], ALU.subtract).then_inc(z_ok, 1)
                if has(k - 1):
                    dve.wait_ge(e_ok, k)
                    V.tensor_tensor(ex[:, jp % 2, 1, :, :], ex[:, jp % 2, 0, :, :], xg[:, jp, :, 0:D], ALU.mult)\
                        .then_inc(msg_ok, 1)
                if has(k - 2):
                    dve.wait_ge(scaled, k - 1)
                    dve.wait_ge(sum_ps_ok, k - 1)
                    V.tensor_tensor(sums, sums, ps_sum[j % 2][:, 0:2 * P], ALU.add).then_inc(acc_ok, 1)

            def early(t, j):
                if j % (SLOTS // EARLY_EACH) == 0:
                    at = ((t - EARLY_TURN) * EARLY_EACH + j * EARLY_EACH // SLOTS) * (2 * P)
                    den = acc_all[:, bass.ds(at, P)]
                    V.reciprocal(den, den).then_inc(early_ok, 1)

            steps(body, dve, 3, 2, early)

            n_fin = [0]

            def done(ins):
                n_fin[0] += 1
                ins.then_inc(fin, 1)
                dve.wait_ge(fin, n_fin[0])

            dve.wait_ge(acc_ok, STEPS)
            done(V.memset(acc_all[:, SPARE:SPARE + 1], 1.0))

            def reciprocals(c):
                first = max(c * CH, EARLY_BLOCKS)
                if first < (c + 1) * CH:
                    den = acc_v[:, first:(c + 1) * CH, 0, :]
                    V.reciprocal(den, den).then_inc(recip_ok, 1)

            reciprocals(0)
            reciprocals(1)
            reciprocals(2)
            for c in range(CH):
                if c + 3 < CH:
                    reciprocals(c + 3)
                dve.wait_ge(o_ps, c + 1)
                if c >= 2:
                    dve.wait_ge(y_ok, c - 1)
                for b in range(CH):
                    last = V.bn_stats(stats[:, b, :], ps_y[c % 3][b // QUAD][:, (b % QUAD) * D:(b % QUAD + 1) * D])
                done(last)
                for b in range(CH):
                    last = V.bn_aggr(mv[:, c % 2, b, :], stats[:, b, :])
                last.then_inc(var_ok, 1)
                dve.wait_ge(std_ok, c + 1)
                done(V.reciprocal(rstd[:, c % 2, :], std[:, c % 2, :]))
                V.scalar_tensor_tensor(out=shift[:, c % 2, :], in0=mv[:, c % 2, :, 0], scalar=-1.0,
                                       in1=rstd[:, c % 2, :], op0=ALU.mult, op1=ALU.mult).then_inc(shift_ok, 1)


_OUTS = [((6250, 128), "float32")]


def kernel(x, src, dst, edge_attr_128, L0_gnn_Wl, L0_gnn_bl, L0_gnn_Wr, L0_gnn_br):
    import numpy as np
    import concourse.bacc as bacc
    from concourse import mybir
    from concourse.bass_utils import run_bass_kernel_spmd

    nc = bacc.Bacc("TRN2", target_bir_lowering=False, num_devices=1)
    given = {"x_in": x, "src_in": src, "dst_in": dst, "edge_attr_in": edge_attr_128, "w_left": L0_gnn_Wl,
             "b_left": L0_gnn_bl, "w_right": L0_gnn_Wr, "b_right": L0_gnn_br}
    arrays = {n: np.ascontiguousarray(a) for n, a in given.items()}
    args = [nc.dram_tensor(n, a.shape, mybir.dt.from_np(a.dtype), kind="ExternalInput").ap()
            for n, a in arrays.items()]
    out = nc.dram_tensor("out", (6250, 128), mybir.dt.float32, kind="ExternalOutput").ap()
    build_gnn_layer(nc, *args, out)
    r = run_bass_kernel_spmd(nc, [arrays], core_ids=[0])
    return r.results[0]["out"]
```

```python
def build_gnn_layer(nc, x, src, dst, edge_attr, w_left, b_left, w_right, b_right, out):
    from contextlib import ExitStack
    import concourse.bass as bass
    from concourse import mybir

    f32, i32, bf16 = mybir.dt.float32, mybir.dt.int32, mybir.dt.bfloat16
    f32r = mybir.dt.float32r
    ALU = mybir.AluOpType
    ACT = mybir.ActivationFunctionType

    P = 128
    N, D = x.shape
    E = src.shape[0]
    TILES = 4
    GE = TILES * P
    GROUPS = -(-E // GE)
    BLOCKS = -(-N // P)
    STEPS = GROUPS + BLOCKS - 1
    TAIL = E - (GROUPS - 1) * GE
    TAIL_P = TAIL // TILES
    ROWS_LAST = N - (BLOCKS - 1) * P
    SLOTS = 6
    BIG = 1.0e38
    SLOPE = 0.2
    EPS = 1.0e-5
    HP = GROUPS // 2
    HE = 2 * GE
    MW = GE + 2
    EARLY_TURN = -(-(GROUPS + 3) // SLOTS)
    EARLY_EACH = 2
    EARLY_BLOCKS = len(range(EARLY_TURN * SLOTS, STEPS, SLOTS // EARLY_EACH))
    CH = 7
    QUAD = 4
    QUADS = -(-BLOCKS // QUAD)
    SPARE = (BLOCKS - 1) * 2 * P + P - 1
    assert GROUPS % 2 == 0 and BLOCKS % CH == 0 and HP <= P and D == P and SLOTS % 2 == 0
    assert TAIL % TILES == 0 and ROWS_LAST < P

    rows_dram = nc.dram_tensor("gather_rows", [BLOCKS * P, 2 * D], f32, kind="Internal").ap()
    field_dram = nc.dram_tensor("edge_fields", [GROUPS * P, 2 * TILES], i32, kind="Internal").ap()
    mask_dram = nc.dram_tensor("start_mask", [HP, 2 * MW], bf16, kind="Internal").ap()

    ctx = ExitStack()
    with ctx:
        def sb(name, shape, dt=f32):
            return ctx.enter_context(nc.sbuf_tensor(name, shape, dt))

        def pb(name, dt=f32):
            return ctx.enter_context(nc.psum_tensor(name, [P, 512], dt))

        def sem(name):
            return ctx.enter_context(nc.semaphore(name))

        right_all = sb("right_all", [P, BLOCKS, D])
        acc_all = sb("acc_all", [P, BLOCKS * 2 * P])
        acc_v = acc_all[:, :].rearrange("d (b c n) -> d b c n", b=BLOCKS, c=2)
        xh_all = acc_all[:, :].rearrange("p (b c) -> p b c", b=BLOCKS)

        field = sb("field", [P, SLOTS, 2 * TILES], i32)
        attr = sb("attr", [P, SLOTS, TILES * D])
        mask = sb("mask", [P, SLOTS, MW], bf16)
        xg = sb("xg", [P, SLOTS, TILES, 2 * D])
        gate = sb("gate", [P, SLOTS], i32)
        rel = sb("rel", [P, SLOTS, TILES])
        onehot = sb("onehot", [P, SLOTS, TILES, P], f32r)
        away = sb("away", [P, TILES, P])
        onehotT = sb("onehotT", [P, 2, TILES * P], f32r)
        v = sb("v", [P, TILES * D])
        s = sb("s", [P, 2, TILES, D])
        F = sb("F", [P, 2, GE])
        B = sb("B", [P, GE])
        z = sb("z", [P, GE])
        eT = sb("eT", [P, GE])
        change = sb("change", [P, 2])
        factor = sb("factor", [P, SLOTS])
        ex = sb("ex", [P, 2, 2, TILES, D])
        ident = sb("ident", [P, P])
        ident_r = sb("ident_r", [P, P], f32r)
        ones = sb("ones", [P, P])
        iota_i = sb("iota_i", [P, 256], i32)
        iota_f = sb("iota_f", [P, 256])
        iota_n = iota_f[:, 0:P]
        bias = sb("bias", [P, 2, D])
        both = sb("both", [P, D])
        w_in = sb("w_in", [P, 2, D])
        wT = sb("wT", [P, 2 * D])
        prev_dst = sb("prev_dst", [HP, 2], i32)
        prev_blk = sb("prev_blk", [HP, 2], i32)
        group_id = sb("group_id", [HP, 2], i32)
        first_step = sb("first_step", [HP, 2])
        prev_f = sb("prev_f", [HP, 2])
        blk_f = sb("blk_f", [HP, 2])
        gid_f = sb("gid_f", [HP, 2])
        goes_on = sb("goes_on", [HP, 2])
        column = sb("column", [HP, 2])
        group_f = sb("group_f", [P, STEPS])
        block_f = sb("block_f", [P, STEPS])
        work_f = sb("work_f", [1, 3, STEPS])
        node0 = sb("node0", [P, STEPS + SLOTS])
        tables = sb("tables", [1, 5, STEPS + SLOTS], i32)
        group_t, block_t, column_t, row_t, sums_t = (tables[0:1, i, :] for i in range(5))
        fields = attr[0:HP, 0:4, :].rearrange("p s d -> p (s d)").bitcast(i32)\
            .rearrange("p (r f) -> p r f", f=2 * TILES)
        dst_int = attr[0:HP, 4:6, :].rearrange("p s d -> p (s d)").bitcast(i32)
        src_int = xg[0:HP, 0, :, :].rearrange("p i d -> p (i d)")[:, 0:HE].bitcast(i32)
        dst_f = xg[0:HP, 1, :, :].rearrange("p i d -> p (i d)")[:, 0:HE]
        differs = xg[0:HP, 2, :, :].rearrange("p i d -> p (i d)")[:, 0:HE]
        hits = F[0:HP, :, :]
        marks = s[0:HP, :, :, :].rearrange("p c i n -> p c (i n)")
        mask_prep = sb("mask_prep", [HP, 2, MW], bf16)
        stats = sb("stats", [P, CH, 6])
        mv = sb("mv", [P, 2, CH, 2])
        std = sb("std", [P, 2, CH])
        rstd = sb("rstd", [P, 2, CH])
        shift = sb("shift", [P, 2, CH])
        y = attr[:, 0:4, :].rearrange("p (c s) d -> p c (s d)", c=2)[:, :, 0:CH * D]\
            .rearrange("p c (b d) -> p c b d", b=CH)
        eps = sb("eps", [P, 1])

        ps_ohT = pb("ps_ohT", f32r)
        ps_e, ps_sum0, ps_sum1, ps_u0, ps_u1, ps_sT0, ps_sT1 = (
            pb(n) for n in ("ps_e", "ps_sum0", "ps_sum1", "ps_u0", "ps_u1", "ps_sT0", "ps_sT1"))
        ps_sum = [ps_sum0, ps_sum1]
        ps_u = [ps_u0, ps_u1]
        ps_sT = [ps_sT0, ps_sT1]
        ps_x = [ps_sum0, ps_sum1]
        ps_left = [ps_e, ps_u0]
        ps_right = [ps_u1, ps_sT0]
        ps_sched, ps_w = ps_sT1, ps_sT1
        ps_y = [(ps_e, ps_u0), (ps_u1, ps_sT0), (ps_sT1, ps_sum0), (ps_sum1, ps_ohT.bitcast(f32))]

        c_set = sem("c_set"); c_iota = sem("c_iota"); c_id = sem("c_id"); identr_ok = sem("identr_ok")
        w_in_s = sem("w_in_s"); b_in_s = sem("b_in_s"); x_in = [sem(f"x_in{i}") for i in range(CH)]
        t_in = sem("t_in"); t_set = sem("t_set"); p_in = sem("p_in")
        right_ps = sem("right_ps"); wT_ps = sem("wT_ps"); wT_sb = sem("wT_sb")
        xT_ps = sem("xT_ps"); xT_sb = sem("xT_sb"); h_ps = sem("h_ps"); h_sb = sem("h_sb")
        r_sb = sem("r_sb")
        rows_out = [sem(f"rows_out{i}") for i in range(CH)]; both_ok = sem("both_ok"); tables_out = sem("tables_out")
        dv = sem("dv")
        hits_ok = sem("hits_ok"); sched_ps = sem("sched_ps"); sched_ok = sem("sched_ok")
        tables_ok = sem("tables_ok"); acc_zero = sem("acc_zero")
        field_in = [sem(f"field_in{i}") for i in range(SLOTS)]
        attr_in = [sem(f"attr_in{i}") for i in range(SLOTS)]
        mask_in = [sem(f"mask_in{i}") for i in range(SLOTS)]
        rows_in = [sem(f"rows_in{i}") for i in range(SLOTS)]
        gate_ok = sem("gate_ok"); rel_ok = sem("rel_ok"); away_ok = sem("away_ok"); oh_ok = sem("oh_ok")
        ohT_ps = sem("ohT_ps"); ohT_sb = sem("ohT_sb")
        u_ps = sem("u_ps"); v_ok = sem("v_ok"); s_ok = sem("s_ok"); sT_ps = sem("sT_ps")
        F_ok = sem("F_ok"); B_ok = sem("B_ok"); z_ok = sem("z_ok"); change_ok = sem("change_ok")
        eT_ok = sem("eT_ok"); factor_ok = sem("factor_ok"); e_ps = sem("e_ps"); e_ok = sem("e_ok")
        msg_ok = sem("msg_ok"); sum_ps_ok = sem("sum_ps_ok"); scaled = sem("scaled"); acc_ok = sem("acc_ok")
        xf_in = [sem(f"xf_in{i}") for i in range(SLOTS)]
        spare_set = sem("spare_set"); early_ok = sem("early_ok"); recip_ok = sem("recip_ok"); ratio_ok = sem("ratio_ok")
        o_ps = sem("o_ps"); stats_ok = sem("stats_ok"); rstd_ok = sem("rstd_ok"); shift_ok = sem("shift_ok")
        y_ok = sem("y_ok"); var_ok = sem("var_ok"); std_ok = sem("std_ok")
        out_s = [sem("out_s0"), sem("out_s1")]

        xf = [xg[:, c, :, :].rearrange("p i d -> p (i d)")[:, 0:CH * D]
              .rearrange("p (b d) -> p b d", b=CH) for c in range(SLOTS)]

        TURNS = STEPS // SLOTS - 1

        def steps(body, eng, before, after, early=None):
            if early:
                parts = ((1, EARLY_TURN, None), (EARLY_TURN, TURNS, early))
            else:
                parts = ((1, TURNS, None),)
            for k in range(-before, SLOTS):
                body(k, k // SLOTS, k % SLOTS)
            for first, last, more in parts:
                with eng.Fori(first, last) as t:
                    for j in range(SLOTS):
                        body(t * SLOTS + j, t, j)
                        if more:
                            more(t, j)
            for k in range(TURNS * SLOTS, STEPS + after):
                body(k, k // SLOTS, k % SLOTS)
                if early and k < STEPS:
                    early(k // SLOTS, k % SLOTS)

        def has(k):
            return not isinstance(k, int) or 0 <= k < STEPS

        def later(k, n):
            return not isinstance(k, int) or k >= n

        def turn(t, j, each):
            return (t + j // SLOTS) * each + each

        def empty(eng, c):
            eng.memset(acc_v[:, c * CH:(c + 1) * CH, 0, :], 1.0e-30)
            eng.memset(acc_v[:, c * CH:(c + 1) * CH, 1, :], 0.0).then_inc(acc_zero, 1)

        block = ctx.enter_context(nc.Block())

        @block.sync
        def _(sp):
            sp.dma_start(w_in[:, 0, :], w_left).then_inc(w_in_s, 16)
            sp.dma_start(w_in[:, 1, :], w_right).then_inc(w_in_s, 16)
            for h, b_in in ((0, b_left), (1, b_right)):
                sp.dma_start(bias[:, h, :], b_in.rearrange("(a n) -> a n", a=1).broadcast_to([P, D]))\
                    .then_inc(b_in_s, 16)
            for c in range(CH):
                b0, b1 = c * CH, min((c + 1) * CH, BLOCKS - 1)
                if c == CH - 1:
                    sp.wait_ge(c_set, 1)
                    sp.dma_start(xh_all[0:ROWS_LAST, BLOCKS - 1, 0:D], x[(BLOCKS - 1) * P:N, :])\
                        .then_inc(x_in[c], 16)
                sp.dma_start(xh_all[:, b0:b1, 0:D],
                             x[b0 * P:b1 * P, :].rearrange("(b p) d -> p b d", p=P)).then_inc(x_in[c], 16)
            for c in range(CH):
                sp.wait_ge(h_sb, -(-CH * (c + 1) // QUAD))
                sp.dma_start(rows_dram[c * CH * P:(c + 1) * CH * P, :].rearrange("(b p) d -> p b d", p=P),
                             xh_all[:, c * CH:(c + 1) * CH, :]).then_inc(rows_out[c], 16)
            sp.wait_ge(tables_out, 32)
            sp.wait_ge(sched_ok, 1)

            def fields_of(k, j):
                g = sp.value_load(group_t[:, bass.ds(k, 1)], min_val=0, max_val=GROUPS - 1)
                sp.dma_start(field[:, j, :], field_dram[bass.ds(g * P, P), :]).then_inc(field_in[j], 16)

            def loads(k, t, j):
                if has(k + 2):
                    jn = (j + 2) % SLOTS
                    if later(k + 2, SLOTS):
                        sp.wait_ge(oh_ok, k + 3 - SLOTS)
                        sp.wait_ge(gate_ok, k + 3 - SLOTS)
                        sp.wait_ge(rows_in[jn], turn(t, j + 2 - SLOTS, 64))
                    fields_of(k + 2, jn)
                if not has(k):
                    return
                g = sp.value_load(group_t[:, bass.ds(k, 1)], min_val=0, max_val=GROUPS - 1)
                r = sp.value_load(row_t[:, bass.ds(k, 1)], min_val=0, max_val=E - (GE - TAIL))
                if later(k, SLOTS):
                    sp.wait_ge(v_ok, k - SLOTS + 1)
                sp.dma_start(attr[0:TAIL_P, j, :],
                             edge_attr[bass.ds(g * GE, TAIL), :].rearrange("(p i) d -> p (i d)", i=TILES))\
                    .then_inc(attr_in[j], 16)
                sp.dma_start(attr[TAIL_P:P, j, :],
                             edge_attr[bass.ds(r, GE - TAIL), :].rearrange("(p i) d -> p (i d)", i=TILES))\
                    .then_inc(attr_in[j], 16)
                if later(k, SLOTS):
                    sp.wait_ge(B_ok, k - SLOTS + 1)
                m = mask_dram.rearrange("p (h e) -> (p h) e", h=2)[bass.ds(g, 1), :]
                sp.dma_start(mask[:, j, :], m.broadcast_to([P, MW])).then_inc(mask_in[j], 16)

            steps(loads, sp, 2, 0)

            sp.wait_ge(msg_ok, STEPS)
            for c in range(CH):
                b0, b1 = c * CH, min((c + 1) * CH, BLOCKS - 1)
                if c >= SLOTS:
                    sp.wait_ge(o_ps, c - SLOTS + 1)
                if c == CH - 1:
                    sp.dma_start(xf[c % SLOTS][0:ROWS_LAST, CH - 1, :], x[(BLOCKS - 1) * P:N, :])\
                        .then_inc(xf_in[c % SLOTS], 16)
                sp.dma_start(xf[c % SLOTS][:, 0:b1 - b0, :],
                             x[b0 * P:b1 * P, :].rearrange("(b p) d -> p b d", p=P)).then_inc(xf_in[c % SLOTS], 16)

        @block.gpsimd
        def _(pool):
            nc.gpsimd.memset(xh_all[:, BLOCKS - 1, :], 0.0).then_inc(c_set, 1)
            nc.gpsimd.memset(ident[:, :], 0.0).then_inc(c_id, 1)
            pool.wait_ge(c_id, 1)
            nc.gpsimd.affine_select(out=ident[:, :], in_=ident[:, :], compare_op=ALU.not_equal, fill=1.0,
                                    base=0, pattern=[[-1, P]], channel_multiplier=1).then_inc(c_id, 1)
            nc.gpsimd.memset(ones[:, :], 1.0).then_inc(c_id, 1)
            nc.gpsimd.iota(iota_i[:, :], [[1, 256]], base=0, channel_multiplier=0).then_inc(c_iota, 1)
            nc.gpsimd.iota(group_id[:, :], [[1, 2]], base=0, channel_multiplier=2).then_inc(c_iota, 1)
            pool.wait_ge(t_set, 3)
            whole = (HP - 1) * HE
            for t, a in ((dst_int[:, :], dst), (src_int, src)):
                pool.dma_start(t[0:HP - 1, :], a[0:whole].rearrange("(p e) -> p e", e=HE)).then_inc(t_in, 16)
                pool.dma_start(t[HP - 1:HP, 0:E - whole],
                               a[whole:E].rearrange("(a e) -> a e", a=1)).then_inc(t_in, 16)
            pool.dma_start(prev_dst[1:HP, 0:1], dst[0:whole].rearrange("(p e) -> p e", e=HE)[:, HE - 1:HE],
                           allow_slow_non_contiguous=True).then_inc(p_in, 16)
            for c in range(CH):
                pool.wait_ge(rows_out[c], 16)
                if c < CH - 1:
                    empty(nc.gpsimd, c)

            def gathers(k, t, j):
                if not has(k):
                    return
                pool.wait_ge(field_in[j], turn(t, j, 16))
                if later(k, SLOTS):
                    pool.wait_ge(msg_ok, k - SLOTS + 1)
                nc.gpsimd.tensor_tensor(gate[:, j:j + 1], field[:, j, 0:1], field[:, j, 0:1], ALU.add)\
                    .then_inc(gate_ok, 1)
                for i in range(TILES):
                    pool.indirect_dma_start(
                        out=xg[:, j, i, :], out_offset=None, in_=rows_dram,
                        in_offset=bass.IndirectOffsetOnAxis(ap=field[:, j, i:i + 1], axis=0),
                    ).then_inc(rows_in[j], 16)

            steps(gathers, pool, 0, 0)

            for c in range(CH):
                den, num = (acc_v[:, c * CH:(c + 1) * CH, i, :] for i in range(2))
                pool.wait_ge(acc_ok, GROUPS - 1 + (c + 1) * CH)
                pool.wait_ge(early_ok, min((c + 1) * CH, EARLY_BLOCKS))
                if (c + 1) * CH > EARLY_BLOCKS:
                    pool.wait_ge(recip_ok, c + 1 - EARLY_BLOCKS // CH)
                nc.gpsimd.tensor_tensor(num, num, den, ALU.mult).then_inc(ratio_ok, 1)

        @block.tensor
        def _(pe):
            pe.wait_ge(c_id, 3)
            pe.wait_ge(w_in_s, 32)
            for h in range(2):
                nc.tensor.transpose(ps_w[:, h * D:(h + 1) * D], w_in[:, h, :], ident[:, :]).then_inc(wT_ps, 1)

            def flip(q):
                blocks = range(q * QUAD, min((q + 1) * QUAD, BLOCKS))
                c = blocks[-1] // CH
                pe.wait_ge(x_in[c], 16 + 16 * (c == CH - 1))
                if q >= 2:
                    pe.wait_ge(xT_sb, q - 1)
                for b in blocks:
                    last = nc.tensor.transpose(ps_x[q % 2][:, (b % QUAD) * P:(b % QUAD + 1) * P],
                                               xh_all[:, b, 0:D], ident[:, :])
                last.then_inc(xT_ps, 1)

            def schedule():
                pe.wait_ge(hits_ok, 4)
                for h, table in ((0, hits), (1, marks)):
                    for c in range(2):
                        last = nc.tensor.matmul(ps_sched[:, h * 256:h * 256 + STEPS], ones[0:HP, :], table[:, c, 0:STEPS],
                                                start=(c == 0), stop=(c == 1))
                last.then_inc(sched_ps, 1)

            flip(0)
            pe.wait_ge(wT_sb, 1)
            for q in range(QUADS):
                if q + 1 < QUADS:
                    flip(q + 1)
                pe.wait_ge(xT_sb, q + 1)
                if q >= 2:
                    pe.wait_ge(h_sb, q - 1)
                for i in range(min(QUAD, BLOCKS - q * QUAD)):
                    last = nc.tensor.matmul(ps_left[q % 2][:, i * D:(i + 1) * D], right_all[:, q * QUAD + i, :],
                                            wT[:, 0:D], start=True, stop=True)
                last.then_inc(h_ps, 1)
            schedule()
            for q in range(QUADS):
                if q >= 2:
                    pe.wait_ge(r_sb, q - 1)
                for i in range(min(QUAD, BLOCKS - q * QUAD)):
                    last = nc.tensor.matmul(ps_right[q % 2][:, i * D:(i + 1) * D], right_all[:, q * QUAD + i, :],
                                            wT[:, D:2 * D], start=True, stop=True)
                last.then_inc(right_ps, 1)
            pe.wait_ge(h_sb, QUADS)
            pe.wait_ge(r_sb, QUADS)
            pe.wait_ge(sched_ok, 1)
            pe.wait_ge(identr_ok, 1)

            sT_view = [bank[:, :].rearrange("d (p i) -> d i p", i=TILES) for bank in ps_sT]
            eT_view = eT[:, :].rearrange("d (p i) -> d i p", i=TILES)

            def body(k, t, j):
                jb, j1, j2, j3 = ((j + n) % SLOTS for n in (-2, 1, 2, 3))
                if has(k + 2):
                    u = ps_u[j % 2]
                    if later(k, 0):
                        pe.wait_ge(v_ok, k + 1)
                    pe.wait_ge(rows_in[j2], turn(t, j + 2, 64))
                    nc.tensor.matmul(u[:, :], ident[:, :], xg[:, j2, :, D:2 * D], start=True, stop=False)
                    b = pe.value_load(block_t[:, bass.ds(k + 2, 1)], min_val=0, max_val=BLOCKS - 1)
                    pe.wait_ge(ohT_sb, k + 3)
                    for i in range(TILES):
                        last = nc.tensor.matmul(u[:, i * D:(i + 1) * D], onehotT[:, j % 2, i * P:(i + 1) * P].bitcast(f32),
                                                right_all[:, bass.ds(b, 1), :].rearrange("p a d -> p (a d)"),
                                                start=False, stop=(i == TILES - 1))
                    last.then_inc(u_ps, 1)
                if has(k - 2):
                    pe.wait_ge(msg_ok, k - 1)
                    if later(k, 4):
                        pe.wait_ge(acc_ok, k - 3)
                    for c in range(2):
                        for i in range(TILES):
                            last = nc.tensor.matmul(ps_sum[j % 2][:, c * P:(c + 1) * P], ex[:, j % 2, c, i, :],
                                                    onehot[:, jb, i, :].bitcast(f32), start=(i == 0), stop=(i == TILES - 1))
                    last.then_inc(sum_ps_ok, 1)
                if has(k + 1):
                    pe.wait_ge(s_ok, k + 2)
                    for i in range(TILES):
                        last = nc.tensor.transpose(sT_view[j1 % 2][:, i, :], s[:, j1 % 2, i, :], ident[:, :])
                    last.then_inc(sT_ps, 1)
                if has(k + 3):
                    pe.wait_ge(oh_ok, k + 4)
                    for i in range(TILES):
                        last = nc.tensor.transpose(ps_ohT[:, i * P:(i + 1) * P], onehot[:, j3, i, :], ident_r[:, :])
                    last.then_inc(ohT_ps, 1)
                if has(k):
                    pe.wait_ge(eT_ok, k + 1)
                    for i in range(TILES):
                        last = nc.tensor.transpose(ps_e[:, i * D:(i + 1) * D], eT_view[:, i, :], ident[:, :])
                    last.then_inc(e_ps, 1)

            steps(body, pe, 3, 2)

            for c in range(CH):
                pe.wait_ge(xf_in[c % SLOTS], 16 * (c // SLOTS + 1) + 16 * (c == CH - 1))
                if c == 2:
                    pe.wait_ge(acc_ok, STEPS)
                if c >= 4:
                    pe.wait_ge(y_ok, c - 3)
                for bank, b0, n in zip(ps_y[c % 4], (0, QUAD), (QUAD, CH - QUAD)):
                    nc.tensor.matmul(bank[:, 0:n * D], ident[:, :], xf[c % SLOTS][:, b0:b0 + n, :], start=True, stop=False)
                    if b0 == 0:
                        pe.wait_ge(ratio_ok, c + 1)
                    for i in range(n):
                        last = nc.tensor.matmul(bank[:, i * D:(i + 1) * D], acc_v[:, c * CH + b0 + i, 1, :],
                                                ident[:, :], start=False, stop=(i == n - 1))
                last.then_inc(o_ps, 1)

        @block.scalar
        def _(act):
            act.wait_ge(wT_ps, 2)
            nc.scalar.activation(wT[:, :], ps_w[:, 0:2 * D], ACT.Copy).then_inc(wT_sb, 1)

            def turned(q):
                n = min(QUAD, BLOCKS - q * QUAD)
                act.wait_ge(xT_ps, q + 1)
                nc.scalar.activation(right_all[:, q * QUAD:q * QUAD + n, :],
                                     ps_x[q % 2][:, 0:n * P].rearrange("p (i n) -> p i n", i=n),
                                     ACT.Copy).then_inc(xT_sb, 1)

            turned(0)
            for q in range(QUADS):
                if q + 1 < QUADS:
                    turned(q + 1)
                n = min(QUAD, BLOCKS - q * QUAD)
                act.wait_ge(h_ps, q + 1)
                nc.scalar.activation(xh_all[:, q * QUAD:q * QUAD + n, D:2 * D],
                                     ps_left[q % 2][:, 0:n * D].rearrange("p (i d) -> p i d", i=n),
                                     ACT.Copy).then_inc(h_sb, 1)
                if q == 6:
                    act.wait_ge(tables_ok, 1)
                    act.dma_start(field_dram.rearrange("(p r) f -> p r f", p=HP), fields[:, :, :]).then_inc(tables_out, 16)
                    act.dma_start(mask_dram, mask_prep[:, :, :].rearrange("p h e -> p (h e)")).then_inc(tables_out, 16)

            def body(k, t, j):
                j3 = (j + 3) % SLOTS
                if has(k - 1):
                    act.wait_ge(e_ps, k)
                    if later(k, 3):
                        act.wait_ge(sum_ps_ok, k - 2)
                    nc.scalar.activation(ex[:, (j + 1) % 2, 0, :, :].rearrange("p i d -> p (i d)"), ps_e[:, :],
                                         ACT.Copy).then_inc(e_ok, 1)
                if has(k + 3):
                    act.wait_ge(field_in[j3], turn(t, j + 3, 16))
                    nc.scalar.activation(rel[:, j3, :], field[:, j3, TILES:2 * TILES].bitcast(f32), ACT.Identity,
                                         bias=node0[:, bass.ds(k + 3, 1)], scale=-1.0).then_inc(rel_ok, 1)
                if has(k - 3):
                    c = act.value_load(column_t[:, bass.ds(k - 3, 1)], min_val=0, max_val=SPARE)
                    pair = acc_all[:, bass.ds(c, 2, P)]
                    if later(k, 4):
                        act.wait_ge(acc_ok, k - 3)
                    else:
                        act.wait_ge(acc_zero, CH)
                    nc.scalar.activation(pair, pair, ACT.Copy, scale=factor[:, j3:j3 + 1]).then_inc(scaled, 1)
                if has(k + 3):
                    act.wait_ge(rel_ok, k + 4)
                    for i in range(TILES):
                        last = nc.scalar.activation(away[:, i, :], iota_n, ACT.Abs, bias=rel[:, j3, i:i + 1])
                    last.then_inc(away_ok, 1)
                    act.wait_ge(away_ok, k + 4)
                    nc.scalar.activation(onehot[:, j3, :, :], away[:, :, :], ACT.Relu, bias=ones[:, 0:1], scale=-1.0)\
                        .then_inc(oh_ok, 1)
                if has(k):
                    act.wait_ge(z_ok, k + 1)
                    if later(k, 1):
                        act.wait_ge(e_ps, k)
                    nc.scalar.activation(eT[:, :], z[:, :], ACT.Exp).then_inc(eT_ok, 1)
                    act.wait_ge(change_ok, k + 1)
                    if later(k, SLOTS):
                        act.wait_ge(scaled, k + 1 - SLOTS)
                    nc.scalar.activation(factor[:, j:j + 1], change[:, j % 2:j % 2 + 1], ACT.Exp)\
                        .then_inc(factor_ok, 1)
                if has(k + 3):
                    act.wait_ge(ohT_ps, k + 4)
                    nc.scalar.activation(onehotT[:, j3 % 2, :], ps_ohT[:, :], ACT.Copy).then_inc(ohT_sb, 1)

            act.wait_ge(c_iota, 2)
            act.wait_ge(c_id, 3)
            nc.scalar.activation(ident_r[:, :], ident[:, :], ACT.Copy).then_inc(identr_ok, 1)
            act.wait_ge(sched_ok, 1)
            steps(body, act, 3, 3)

            def results(c):
                act.wait_ge(shift_ok, c + 1)
                if c >= 2:
                    act.wait_ge(out_s[c % 2], 16 * (c // 2))
                for b in range(CH):
                    last = nc.scalar.activation(y[:, c % 2, b, :],
                                                ps_y[c % 4][b // QUAD][:, (b % QUAD) * D:(b % QUAD + 1) * D],
                                                ACT.Identity, bias=shift[:, c % 2, b:b + 1], scale=rstd[:, c % 2, b:b + 1])
                last.then_inc(y_ok, 1)
                act.wait_ge(y_ok, c + 1)
                b0, b1 = c * CH, min((c + 1) * CH, BLOCKS - 1)
                if c == CH - 1:
                    act.dma_start(out[(BLOCKS - 1) * P:N, :], y[0:ROWS_LAST, c % 2, CH - 1, :])\
                        .then_inc(out_s[c % 2], 16)
                act.dma_start(out[b0 * P:b1 * P, :].rearrange("(b p) d -> p b d", p=P),
                              y[:, c % 2, 0:b1 - b0, :]).then_inc(out_s[c % 2], 16)

            for c in range(CH):
                act.wait_ge(var_ok, c + 1)
                nc.scalar.activation(std[:, c % 2, :], mv[:, c % 2, :, 1], ACT.Sqrt, bias=eps[:, 0:1]).then_inc(std_ok, 1)
                results(c)
            act.wait_ge(out_s[0], 16 * 5)
            act.wait_ge(out_s[1], 16 * 3)

        @block.vector
        def _(dve):
            n_dv = [0]

            def chained(ins):
                n_dv[0] += 1
                ins.then_inc(dv, 1)
                dve.wait_ge(dv, n_dv[0])

            V = nc.vector
            V.memset(dst_int[:, :], -1).then_inc(t_set, 1)
            V.memset(src_int, 0).then_inc(t_set, 1)
            V.memset(prev_dst[:, :], 0).then_inc(t_set, 1)
            V.memset(eps[:, :], EPS)
            V.memset(F[:, 1, GE - 1:GE], -BIG)

            dve.wait_ge(b_in_s, 32)
            V.tensor_tensor(both[:, :], bias[:, 0, :], bias[:, 1, :], ALU.add).then_inc(both_ok, 1)
            dve.wait_ge(both_ok, 1)

            def rights(q):
                n = min(QUAD, BLOCKS - q * QUAD)
                dve.wait_ge(right_ps, q + 1)
                V.tensor_tensor(right_all[:, q * QUAD:q * QUAD + n, :],
                                ps_right[q % 2][:, 0:n * D].rearrange("p (i d) -> p i d", i=n),
                                both[:, None, :].broadcast_to([P, n, D]), ALU.add).then_inc(r_sb, 1)

            dve.wait_ge(t_in, 64)
            dve.wait_ge(p_in, 16)
            fv = fields[:, :, :].rearrange("p r (f i) -> p r f i", f=2)
            quad = lambda a: a.rearrange("p (r i) -> p r i", i=TILES)
            V.tensor_copy(fv[:, :, 0, :], quad(src_int))
            chained(V.tensor_copy(prev_dst[:, 1:2], dst_int[:, GE - 1:GE]))
            V.tensor_copy(prev_f[:, :], prev_dst[:, :])
            chained(V.tensor_copy(dst_f, dst_int[:, :]))
            V.tensor_copy(fv[:, :, 1, :].bitcast(f32), quad(dst_f))
            V.tensor_tensor(differs[:, 1:HE], dst_f[:, 0:HE - 1], dst_f[:, 1:HE], ALU.not_equal)
            chained(V.tensor_tensor(differs[:, 0:1], prev_f[:, 0:1], dst_f[:, 0:1], ALU.not_equal))
            V.memset(mask_prep[:, :, GE:MW], 0.0)
            V.tensor_scalar(mask_prep[:, :, 0:GE], differs.rearrange("p (h e) -> p h e", h=2), -BIG, None, ALU.mult)\
                .then_inc(tables_ok, 1)

            dve.wait_ge(c_iota, 2)
            V.tensor_copy(iota_f[:, :], iota_i[:, :])
            V.tensor_copy(gid_f[:, :], group_id[:, :])
            chained(V.tensor_scalar(prev_blk[:, :], prev_dst[:, :], 7, None, ALU.arith_shift_right))
            chained(V.tensor_copy(blk_f[:, :], prev_blk[:, :]))
            V.tensor_tensor(first_step[:, :], gid_f[:, :], blk_f[:, :], ALU.add)
            V.tensor_scalar(goes_on[:, :], differs.rearrange("p (h e) -> p h e", h=2)[:, :, 0], -1.0, 1.0,
                            ALU.mult, ALU.add)
            chained(V.scalar_tensor_tensor(out=column[:, :], in0=blk_f[:, :], scalar=float(P), in1=prev_f[:, :],
                                           op0=ALU.mult, op1=ALU.add))
            chained(V.scalar_tensor_tensor(out=column[:, :], in0=column[:, :], scalar=-float(SPARE),
                                           in1=goes_on[:, :], op0=ALU.add, op1=ALU.mult))
            for c in range(2):
                V.tensor_scalar(hits[:, c, 0:STEPS], iota_f[0:HP, 0:STEPS], first_step[:, c:c + 1], None,
                                ALU.is_ge).then_inc(hits_ok, 1)
                V.tensor_scalar(marks[:, c, 0:STEPS], iota_f[0:HP, 0:STEPS], first_step[:, c:c + 1],
                                column[:, c:c + 1], ALU.is_equal, ALU.mult).then_inc(hits_ok, 1)

            dve.wait_ge(sched_ps, 1)
            chained(V.tensor_scalar(group_f[:, :], ps_sched[:, 0:STEPS], -1.0, None, ALU.add))
            V.tensor_scalar(work_f[:, 0, :], group_f[0:1, :], float(GE), float(TAIL), ALU.mult, ALU.add)
            V.tensor_scalar(work_f[:, 1, :], ps_sched[0:1, 256:256 + STEPS], float(SPARE), None, ALU.add)
            chained(V.tensor_tensor(block_f[:, :], iota_f[:, 0:STEPS], group_f[:, :], ALU.subtract))
            V.tensor_scalar(node0[:, 0:STEPS], block_f[:, :], float(P), None, ALU.mult)
            V.tensor_copy(group_t[:, 0:STEPS], group_f[0:1, :])
            V.tensor_copy(block_t[:, 0:STEPS], block_f[0:1, :])
            V.tensor_scalar(sums_t[:, 0:STEPS], block_f[0:1, :], float(2 * P), None, ALU.mult)
            V.tensor_copy(column_t[:, 0:STEPS], work_f[:, 1, :])
            chained(V.tensor_scalar(work_f[:, 2, :], work_f[:, 0, :], float(E - (GE - TAIL)), None, ALU.min))
            chained(V.tensor_copy(row_t[:, 0:STEPS], work_f[:, 2, :]))
            V.memset(change[:, :], 0.0).then_inc(sched_ok, 1)

            for q in range(QUADS):
                rights(q)

            dve.wait_ge(rows_out[CH - 1], 16)
            empty(V, CH - 1)
            dve.wait_ge(acc_zero, CH)
            dve.wait_ge(sched_ok, 1)

            def body(k, t, j):
                j1, jp = (j + 1) % SLOTS, (j - 1) % SLOTS
                if has(k + 1):
                    if later(k, 0):
                        dve.wait_ge(s_ok, k + 1)
                    dve.wait_ge(attr_in[j1], turn(t, j + 1, 32))
                    dve.wait_ge(u_ps, k + 2)
                    V.tensor_tensor(v[:, :], ps_u[j1 % 2][:, :], attr[:, j1, :], ALU.mult).then_inc(v_ok, 1)
                if has(k):
                    dve.wait_ge(mask_in[j], turn(t, j, 16))
                    dve.wait_ge(sT_ps, k + 1)
                    if later(k, 1):
                        dve.wait_ge(change_ok, k)
                    V.tensor_tensor_scan(F[:, j % 2, :], mask[:, j, 0:GE], ps_sT[j % 2][:, :],
                                         F[:, (j - 1) % 2, GE - 1:GE], ALU.add, ALU.max).then_inc(F_ok, 1)
                if has(k + 1):
                    dve.wait_ge(v_ok, k + 2)
                    V.scalar_tensor_tensor(out=s[:, j1 % 2, :, :].rearrange("p i d -> p (i d)"), in0=v[:, :],
                                           scalar=SLOPE, in1=v[:, :], op0=ALU.mult, op1=ALU.max).then_inc(s_ok, 1)
                if has(k - 3):
                    at = dve.value_load(sums_t[:, bass.ds(k - 3, 1)], min_val=0, max_val=(BLOCKS - 1) * 2 * P)
                    sums = acc_all[:, bass.ds(at, 2 * P)]
                if has(k):
                    dve.wait_ge(F_ok, k + 1)
                    V.tensor_tensor_scan(B[:, ::-1], mask[:, j, GE:0:-1], F[:, j % 2, ::-1], -BIG,
                                         ALU.add, ALU.max).then_inc(B_ok, 1)
                if has(k - 1):
                    dve.wait_ge(e_ok, k)
                    V.tensor_tensor(ex[:, jp % 2, 1, :, :], ex[:, jp % 2, 0, :, :], xg[:, jp, :, 0:D], ALU.mult)\
                        .then_inc(msg_ok, 1)
                if has(k):
                    dve.wait_ge(B_ok, k + 1)
                    if later(k, 1):
                        dve.wait_ge(eT_ok, k)
                    V.tensor_tensor(z[:, :], ps_sT[j % 2][:, :], B[:, :], ALU.subtract).then_inc(z_ok, 1)
                if has(k):
                    dve.wait_ge(B_ok, k + 1)
                    V.tensor_scalar(change[:, j % 2:j % 2 + 1], F[:, (j - 1) % 2, GE - 1:GE], B[:, 0:1], 0.0,
                                    ALU.subtract, ALU.min).then_inc(change_ok, 1)
                if has(k - 3):
                    dve.wait_ge(scaled, k - 2)
                    dve.wait_ge(sum_ps_ok, k - 2)
                    V.tensor_tensor(sums, sums, ps_sum[(j - 3) % 2][:, 0:2 * P], ALU.add).then_inc(acc_ok, 1)
                if isinstance(k, int) and k == STEPS:
                    for c in range(3):
                        reciprocals(c)

            def reciprocals(c, parts=(0, 1)):
                for part in parts:
                    b0, b1 = ((0, CH // 2), (CH // 2, CH))[part]
                    if EARLY_BLOCKS < (c + 1) * CH and c < CH:
                        den = acc_v[:, max(c * CH + b0, EARLY_BLOCKS):c * CH + b1, 0, :]
                        last = V.reciprocal(den, den)
                        if part == 1:
                            last.then_inc(recip_ok, 1)

            def early(t, j):
                if j % (SLOTS // EARLY_EACH) == 0:
                    at = ((t - EARLY_TURN) * EARLY_EACH + j * EARLY_EACH // SLOTS) * (2 * P)
                    den = acc_all[:, bass.ds(at, P)]
                    V.reciprocal(den, den).then_inc(early_ok, 1)

            steps(body, dve, 3, 3, early)

            dve.wait_ge(acc_ok, STEPS)
            V.memset(acc_all[:, SPARE:SPARE + 1], 1.0).then_inc(spare_set, 1)
            dve.wait_ge(spare_set, 1)
            for c in range(CH):
                dve.wait_ge(o_ps, c + 1)
                if c >= 1:
                    dve.wait_ge(var_ok, c)
                for b in range(CH):
                    last = V.bn_stats(stats[:, b, :], ps_y[c % 4][b // QUAD][:, (b % QUAD) * D:(b % QUAD + 1) * D])
                last.then_inc(stats_ok, 1)
                dve.wait_ge(stats_ok, c + 1)
                if c >= 2:
                    dve.wait_ge(y_ok, c - 1)
                    dve.wait_ge(shift_ok, c - 1)
                for b in range(CH):
                    last = V.bn_aggr(mv[:, c % 2, b, :], stats[:, b, :])
                last.then_inc(var_ok, 1)
                reciprocals(c + 3, (0,))
                dve.wait_ge(std_ok, c + 1)
                V.reciprocal(rstd[:, c % 2, :], std[:, c % 2, :]).then_inc(rstd_ok, 1)
                reciprocals(c + 3, (1,))
                dve.wait_ge(rstd_ok, c + 1)
                V.scalar_tensor_tensor(out=shift[:, c % 2, :], in0=mv[:, c % 2, :, 0], scalar=-1.0,
                                       in1=rstd[:, c % 2, :], op0=ALU.mult, op1=ALU.mult).then_inc(shift_ok, 1)


_OUTS = [((6250, 128), "float32")]


def kernel(x, src, dst, edge_attr_128, L0_gnn_Wl, L0_gnn_bl, L0_gnn_Wr, L0_gnn_br):
    import numpy as np
    import concourse.bacc as bacc
    from concourse import mybir
    from concourse.bass_utils import run_bass_kernel_spmd

    nc = bacc.Bacc("TRN2", target_bir_lowering=False, num_devices=1)
    given = {"x_in": x, "src_in": src, "dst_in": dst, "edge_attr_in": edge_attr_128, "w_left": L0_gnn_Wl,
             "b_left": L0_gnn_bl, "w_right": L0_gnn_Wr, "b_right": L0_gnn_br}
    arrays = {n: np.ascontiguousarray(a) for n, a in given.items()}
    args = [nc.dram_tensor(n, a.shape, mybir.dt.from_np(a.dtype), kind="ExternalInput").ap()
            for n, a in arrays.items()]
    out = nc.dram_tensor("out", (6250, 128), mybir.dt.float32, kind="ExternalOutput").ap()
    build_gnn_layer(nc, *args, out)
    r = run_bass_kernel_spmd(nc, [arrays], core_ids=[0])
    return r.results[0]["out"]
```
